# Optimizing a Trainium2 kernel written in Bass

```python
import numpy as np
import jax
import jax.numpy as jnp

def _softmax(x, axis=-1):
    return jax.nn.softmax(x, axis=axis)

def _gelu(x):
    return jax.nn.gelu(x, approximate=True)

def _silu(x):
    return jax.nn.silu(x)

def _sigmoid(x):
    return jax.nn.sigmoid(x)

def _layernorm(x, axis=-1, eps=1e-05):
    m = jnp.mean(x, axis=axis, keepdims=True)
    v = jnp.var(x, axis=axis, keepdims=True)
    return (x - m) / jnp.sqrt(v + eps)

def _scatter_add(tgt, idx, src, axis=0):
    return tgt.at[idx].add(src)

def _segment_sum(src, seg, n):
    return jax.ops.segment_sum(src, seg, n)
kernel_name = 'mk_flamingo_gated_d1_seqx_r2_c77b94'

def setup_inputs(seed: int=0):
    np.random.seed(seed)
    _w = jnp.asarray

    def _rec_inputs():
        import jax
        import jax.numpy as jnp
        _rk = jax.random.key(seed)
        x = -0.0002928 + 1 * jax.random.normal(jax.random.fold_in(_rk, 1), (2, 2048, 512), jnp.float32)
        _lenS = 2048 - jax.random.randint(jax.random.fold_in(_rk, 7), (2,), 0, max(1, 2048 // 4) + 1, jnp.int32)
        _lenS2 = 77 - jax.random.randint(jax.random.fold_in(_rk, 8), (2,), 0, max(1, 77 // 4) + 1, jnp.int32)
        _ctx_1024P = jax.random.normal(jax.random.fold_in(_rk, 11), (2, 16, 512), jnp.float32)
        _ctx_1024c = jax.random.dirichlet(jax.random.fold_in(_rk, 511), 0.3 * jnp.ones((16,), jnp.float32), (2, 77))
        _ctx_1024t = jnp.einsum('bsk,bkd->bsd', _ctx_1024c, _ctx_1024P)
        _ctx_1024t = _ctx_1024t * jax.lax.rsqrt(jnp.mean(jnp.square(_ctx_1024t)) + 1e-12) * 0.953939
        ctx_1024 = -1.39393e-06 + 0.999914 * (_ctx_1024t + 0.3 * jax.random.normal(jax.random.fold_in(_rk, 611), (2, 77, 512), jnp.float32))
        _g = jax.random.normal(jax.random.fold_in(_rk, 9001), (2, 1), jnp.float32)
        _g = jnp.sign(_g) * jnp.maximum(jnp.abs(_g), 1.0) + (_g == 0) * 1.0
        g_xattn = _g[0]
        g_ffn = _g[1]
        return (x, ctx_1024, g_xattn, g_ffn)
    x, ctx_1024, g_xattn, g_ffn = _rec_inputs()

    def _L0_xattn_setup():
        import jax, jax.numpy as jnp
        import numpy as np
        B, S, D, H = (2, 1024, 512, 16)
        HD = D // H
        SCALE = HD ** (-0.5)
        NEG = -1000000000.0
        key = jax.random.key(seed)
        ks = jax.random.split(key, 7)
        w_std = 1.0 / np.sqrt(D)
        return {'query': jax.random.normal(ks[0], (B, S, D), dtype=jnp.float32), 'key': jax.random.normal(ks[1], (B, S, D), dtype=jnp.float32), 'value': jax.random.normal(ks[2], (B, S, D), dtype=jnp.float32), 'Wq': jax.random.normal(ks[3], (D, D), dtype=jnp.float32) * w_std, 'Wk': jax.random.normal(ks[4], (D, D), dtype=jnp.float32) * w_std, 'Wv': jax.random.normal(ks[5], (D, D), dtype=jnp.float32) * w_std, 'Wo': jax.random.normal(ks[6], (D, D), dtype=jnp.float32) * w_std}
    _L0_xattn_all = _L0_xattn_setup()
    _L0_xattn_in = {k: v for k, v in _L0_xattn_all.items() if k in ('Wq', 'Wk', 'Wv', 'Wo')}
    del _L0_xattn_all

    def _L0_ffn_setup():
        import jax, jax.numpy as jnp
        import numpy as np
        DIM = 512
        HIDDEN = 1536
        SCALE = 1.0 / 127.0

        def _dequant(w_int, dtype):
            return w_int.astype(dtype) * jnp.asarray(SCALE, dtype)
        key = jax.random.key(seed)
        k_x, k_g, k_u, k_d = jax.random.split(key, 4)
        x = jax.random.normal(k_x, (4, 1024, DIM), dtype=jnp.float32)
        w_gate = jax.random.randint(k_g, (HIDDEN, DIM), -127, 128, dtype=jnp.int32)
        w_up = jax.random.randint(k_u, (HIDDEN, DIM), -127, 128, dtype=jnp.int32)
        w_down = jax.random.randint(k_d, (DIM, HIDDEN), -127, 128, dtype=jnp.int32)
        return {'x': x, 'w_gate': w_gate, 'w_up': w_up, 'w_down': w_down}
    _L0_ffn_all = _L0_ffn_setup()
    _L0_ffn_in = {k: v for k, v in _L0_ffn_all.items() if k in ('w_gate', 'w_up', 'w_down')}
    del _L0_ffn_all
    return {'x': x, 'ctx_1024': ctx_1024, 'g_xattn': g_xattn, 'g_ffn': g_ffn, 'L0_xattn_Wq': _L0_xattn_in['Wq'], 'L0_xattn_Wk': _L0_xattn_in['Wk'], 'L0_xattn_Wv': _L0_xattn_in['Wv'], 'L0_xattn_Wo': _L0_xattn_in['Wo'], 'L0_ffn_w_gate': _L0_ffn_in['w_gate'], 'L0_ffn_w_up': _L0_ffn_in['w_up'], 'L0_ffn_w_down': _L0_ffn_in['w_down']}

def reference(x, ctx_1024, g_xattn, g_ffn, L0_xattn_Wq, L0_xattn_Wk, L0_xattn_Wv, L0_xattn_Wo, L0_ffn_w_gate, L0_ffn_w_up, L0_ffn_w_down):
    import jax
    import jax.numpy as jnp

    def _L0_xattn_ref(query, key, value, Wq, Wk, Wv, Wo):
        import jax, jax.numpy as jnp
        import numpy as np
        B, S, D, H = (2, 1024, 512, 16)
        HD = D // H
        SCALE = HD ** (-0.5)
        NEG = -1000000000.0
        b, sq, d = query.shape
        sk = key.shape[1]
        q = (query @ Wq.T).reshape(b, sq, H, HD).transpose(0, 2, 1, 3)
        k = (key @ Wk.T).reshape(b, sk, H, HD).transpose(0, 2, 1, 3)
        v = (value @ Wv.T).reshape(b, sk, H, HD).transpose(0, 2, 1, 3)
        scores = jnp.einsum('bhqd,bhkd->bhqk', q, k) * SCALE
        causal = jnp.arange(sq)[:, None] >= jnp.arange(sk)[None, :]
        scores = jnp.where(causal[None, None], scores, NEG)
        attn = jax.nn.softmax(scores, axis=-1)
        out = jnp.einsum('bhqk,bhkd->bhqd', attn, v)
        out = out.transpose(0, 2, 1, 3).reshape(b, sq, d)
        return out @ Wo.T

    def _L0_ffn_ref(x, w_gate, w_up, w_down):
        import jax, jax.numpy as jnp
        import numpy as np
        DIM = 512
        HIDDEN = 1536
        SCALE = 1.0 / 127.0

        def _dequant(w_int, dtype):
            return w_int.astype(dtype) * jnp.asarray(SCALE, dtype)
        wg = _dequant(w_gate, x.dtype)
        wu = _dequant(w_up, x.dtype)
        wd = _dequant(w_down, x.dtype)
        gate = jnp.einsum('bsd,hd->bsh', x, wg)
        up = jnp.einsum('bsd,hd->bsh', x, wu)
        h = jax.nn.silu(gate) * up
        return jnp.einsum('bsh,dh->bsd', h, wd)
    x = x + jnp.tanh(g_xattn[0]) * _L0_xattn_ref(_layernorm(x, axis=-1), ctx_1024, ctx_1024, L0_xattn_Wq, L0_xattn_Wk, L0_xattn_Wv, L0_xattn_Wo)
    x = x + jnp.tanh(g_ffn[0]) * _L0_ffn_ref(_layernorm(x, axis=-1), L0_ffn_w_gate, L0_ffn_w_up, L0_ffn_w_down)
    return x

_drawn_inputs = setup_inputs


def setup_inputs(seed=0):
    import zlib

    import numpy as np

    out = dict(_drawn_inputs(seed))
    spreads = {}
    factors = {}
    for name, (base, spread) in spreads.items():
        noise = np.random.default_rng([zlib.crc32(name.encode()), seed]).standard_normal(out[name].shape)
        drawn = base * np.exp(spread * noise) if base else spread * noise
        out[name] = jnp.asarray(drawn.astype(out[name].dtype))
    for name, factor in factors.items():
        out[name] = (out[name] * factor).astype(out[name].dtype)
    return out
```

```python
import concourse.bass as bass
from concourse import mybir
from contextlib import ExitStack


def flamingo_gated_block(
    nc: bass.Bass,
    x: bass.AP,
    ctx_t: bass.AP,
    g_xattn: bass.AP,
    g_ffn: bass.AP,
    wq_t: bass.AP,
    wk_t: bass.AP,
    wv_t: bass.AP,
    wo_t: bass.AP,
    w_gate_t: bass.AP,
    w_up_t: bass.AP,
    w_down_t: bass.AP,
    x_mid: bass.AP,
    out: bass.AP,
):
    f32, f32r, i32 = mybir.dt.float32, mybir.dt.float32r, mybir.dt.int32
    ALU = mybir.AluOpType
    ACT = mybir.ActivationFunctionType
    AX = mybir.AxisListType

    P = 128
    B, SQ, D = x.shape
    SK = ctx_t.shape[1] // B
    HID = w_gate_t.shape[1]
    H, HD = 16, 32
    SCALE = HD ** -0.5
    NEG = -1e9
    EPS = 1e-5
    W_SCALE = 1.0 / 127.0
    KD = D // P
    TT = 4
    TB = TT * P
    NB = B * SQ // TB
    BPB = SQ // TB
    HG = P // HD
    G = H // HG
    GK = HG * SK
    UH = H // 2
    CH = -(-GK // 3)
    CS = [0, CH, GK - CH]
    NC = 3 * G
    MH = HID // P

    x_f = x.rearrange("b s d -> (b s) d").rearrange("(n t p) d -> n p t d", p=P, t=TT)
    out_f = out.rearrange("b s d -> (b s) d").rearrange("(n t p) d -> n p t d", p=P, t=TT)
    mid_f = x_mid.rearrange("(n t p) d -> n p t d", p=P, t=TT)

    def t_base(n):
        return 4 + 16 * n

    V_AT = 4 + 4
    M_Q1 = V_AT + 6

    def m_base(n):
        return M_Q1 + 4 + 12 * (n - 1) - (4 if isinstance(n, int) and n == NB else 0)

    def h_base(n):
        return 8 + 8 * (n - 1)

    T_P2 = t_base(NB - 1) + 12
    M_LAST = m_base(NB)
    M_P2 = M_LAST + 8
    H_LAST = h_base(NB - 1) + 4

    ctx = ExitStack()
    with ctx:
        def sb(name, shape, dt=f32, where=ctx):
            return where.enter_context(nc.sbuf_tensor(name, shape, dt))

        def sem(name):
            return ctx.enter_context(nc.semaphore(name))

        ident = sb("ident", [P, P])
        causal = sb("causal", [P, HG, SK])
        gates = sb("gates", [P, 2])
        gate_t = sb("gate_t", [P, 2])
        gate_ffn = sb("gate_ffn", [P, 1])
        bn = sb("bn", [P, TT, 6])
        mv = sb("mv", [P, TT, 2])
        rstd = sb("rstd", [P, TT])
        nmean = sb("nmean", [P, TT])
        half = sb("half", [P, TT])
        mx = sb("mx", [P, 2, H])
        nmx = sb("nmx", [P, 2, UH])
        den = sb("den", [P, 2, H])
        rden = sb("rden", [P, 2, H])
        raw = sb("raw", [P, 3, KD, P * 2], i32)

        with ExitStack() as a1:
            wq = sb("wq", [P, 2, KD, D], f32r, a1)
            xT = sb("xT", [P, 2, KD, TB], f32r, a1)
            x_ln = sb("x_ln", [P, TT, D], f32, a1)
            wv_stage = sb("wv_stage", [P, KD, D], f32, a1)
        w_gu = sb("w_gu", [P, KD, 2 * HID], f32r)
        with ExitStack() as b1:
            qT = sb("qT", [P, 2, G, TB], f32r, b1)
            K = sb("K", [P, 2, B, G, GK], f32r, b1)
            e = sb("e", [P, 2, H, SK], f32, b1)
        with ExitStack() as b2:
            x2 = sb("x2", [P, 2, TT, D], f32, b2)
            xh = sb("xh", [P, TT, D], f32, b2)
            xT2 = sb("xT2", [P, 2, KD, TB], f32r, b2)
        sb("region_b", [P, 2 * G * TB + 2 * B * G * GK + 2 * H * SK])
        with ExitStack() as c0:
            wq_stage = sb("wq_stage", [P, KD, D], f32, c0)
            wk_stage = sb("wk_stage", [P, KD, D], f32, c0)
            wo_stage = sb("wo_stage", [P, KD, D], f32, c0)
            ctx_stage = sb("ctx_stage", [P, KD, B * SK], f32, c0)
            k_mask = sb("k_mask", [P, HG, SK], f32, c0)
            k_full = sb("k_full", [P, 2, HG, SK], f32, c0)
        with ExitStack() as c1:
            pT = sb("pT", [P, 2, NC, TB], f32r, c1)
        hT = sb("hT", [P, 2, MH, TB], f32r)
        with ExitStack() as d1:
            V = sb("V", [P, 2, B, NC, P], f32r, d1)
        w_d = sb("w_d", [P, MH, D], f32r)
        with ExitStack() as e0:
            ctx_rep = sb("ctx_rep", [P, KD, B, GK], f32, e0)
            v_mask = sb("v_mask", [P, 3, HG, HD], f32, e0)
            v_full = sb("v_full", [P, 2, G, P], f32, e0)
        with ExitStack() as e2:
            th = sb("th", [P, 2, TB], f32, e2)
            hid = sb("hid", [P, 2, TB], f32, e2)
        aT = sb("aT", [P, 2, G, TB], f32r)
        wo = sb("wo", [P, 2, KD, D], f32r)
        x_res = sb("x_res", [P, TT, D])

        psum = ctx.enter_context(nc.psum_tensor("psum", [P, 8, 512], f32))
        s_bank = [psum[:, 0:2, :], psum[:, 2:4, :]]
        t_bank = [psum[:, 4, :], psum[:, 5, :]]
        m_bank = [psum[:, 6, :], psum[:, 7, :]]

        consts_ready = sem("consts_ready")
        const_step = sem("const_step")
        half_ready = sem("half_ready")
        gates_in = sem("gates_in")
        gates_tanh = sem("gates_tanh")
        gate_ready = sem("gate_ready")
        wq_in, wk_in, wv_in, wo_in = sem("wq_in"), sem("wk_in"), sem("wv_in"), sem("wo_in")
        ctx_in, rep_in = sem("ctx_in"), sem("rep_in")
        w_hi = sem("w_hi")
        w_split = sem("w_split")
        kv_full = sem("kv_full")
        kv_hi = sem("kv_hi")
        x_in = sem("x_in")
        bn_done = sem("bn_done")
        stats_ready = sem("stats_ready")
        var_eps = sem("var_eps")
        rstd_ready = sem("rstd_ready")
        x_normed = sem("x_normed")
        dve_passed, pool_passed = sem("dve_passed"), sem("pool_passed")
        t_full, t_hi, t_free = sem("t_full"), sem("t_hi"), sem("t_free")
        m_full, m_hi, m_free = sem("m_full"), sem("m_hi"), sem("m_free")
        s0_full, s1_full = sem("s0_full"), sem("s1_full")
        mx0_done, mx1_done = sem("mx0_done"), sem("mx1_done")
        s0_shifted = sem("s0_shifted")
        nmx_ready = sem("nmx_ready")
        exp0_done, exp1_done = sem("exp0_done"), sem("exp1_done")
        sum_done = sem("sum_done")
        rden_ready = sem("rden_ready")
        p_ready = sem("p_ready")
        res_in = [sem(f"res_in{t}") for t in range(TT)]
        mid_out = [sem(f"mid_out{t}") for t in range(TT)]
        raw_in = [sem(f"raw_in{i}") for i in range(3)]
        raw_used = sem("raw_used")
        x2_in = [sem(f"x2_in{i}") for i in range(2)]
        bn2_done, stats2_ready = sem("bn2_done"), sem("stats2_ready")
        var2_eps, rstd2_ready = sem("var2_eps"), sem("rstd2_ready")
        x2_normed = sem("x2_normed")
        gu_full, tanh_done, gu_free = sem("gu_full"), sem("tanh_done"), sem("gu_free")
        silu_done = sem("silu_done")
        h_hi, h_lo = sem("h_hi"), sem("h_lo")
        out_done = [sem(f"out_done{i}") for i in range(2)]

        def raw_parts():
            gate = w_gate_t.rearrange("(k p) h -> p k h", p=P)
            up = w_up_t.rearrange("(k p) h -> p k h", p=P)
            down = w_down_t.rearrange("(k p) d -> p k d", p=P)
            parts = []
            for m in range(MH):
                c = slice(m * P, (m + 1) * P)
                parts.append(([(gate[:, :, c], slice(0, P)), (up[:, :, c], slice(P, 2 * P))],
                              w_gu[:, :, 2 * P * m:2 * P * (m + 1)]))
            for m in range(0, MH, 2):
                parts.append(([(down[:, m:m + 2, :], None)], w_d[:, m:m + 2, :]))
            return parts

        PARTS = raw_parts()

        block = ctx.enter_context(nc.Block())

        @block.sync
        def _(sp):
            def load_x(n, first=False):
                if not first:
                    sp.wait_ge(t_full, t_base(n - 2) + 10)
                sp.dma_start(x_ln[:, :, :], x_f[n]).then_inc(x_in, 16)

            def residual(n, first=False, between={}):
                for t in range(TT):
                    if not first:
                        sp.wait_ge(mid_out[t], 16 * (n - 1))
                    sp.dma_start(x_res[:, t, :], x_f[n - 1, :, t, :]).then_inc(res_in[t], 16)
                for i in between.get(-1, []):
                    fetch(i)
                for t in range(TT):
                    sp.wait_ge(m_free, m_base(n) + 5 + t)
                    sp.dma_start(mid_f[n - 1, :, t, :], x_res[:, t, :]).then_inc(mid_out[t], 16)
                    for i in between.get(t, []):
                        fetch(i)

            sp.dma_start(x_ln[:, :, :], x_f[0]).then_inc(x_in, 16)
            sp.dma_start(wq_stage[:, :, :], wq_t.rearrange("(k p) n -> p k n", p=P)).then_inc(wq_in, 16)
            sp.dma_start(ctx_stage[:, :, :], ctx_t.rearrange("(k p) n -> p k n", p=P)).then_inc(ctx_in, 16)
            sp.dma_start(wk_stage[:, :, :], wk_t.rearrange("(k p) n -> p k n", p=P)).then_inc(wk_in, 16)
            sp.dma_start(wv_stage[:, :, :], wv_t.rearrange("(k p) n -> p k n", p=P)).then_inc(wv_in, 16)
            ctx_p = ctx_t.rearrange("(k p) (b s) -> p k b s", p=P, b=B)
            for j in range(HG):
                for b in range(B):
                    sp.dma_start(ctx_rep[:, :, b, j * SK:(j + 1) * SK], ctx_p[:, :, b, :]).then_inc(rep_in, 16)
            sp.dma_start(wo_stage[:, :, :], wo_t.rearrange("(k p) n -> p k n", p=P)).then_inc(wo_in, 16)
            sp.wait_ge(t_full, 4)
            load_x(1, first=True)
            load_x(2)
            residual(1, first=True)
            with sp.Fori(2, NB - 1) as n:
                load_x(n + 1)
                residual(n)

            def fetch(i):
                if i >= 3:
                    sp.wait_ge(raw_used, i - 2)
                srcs, _ = PARTS[i]
                for src, cols in srcs:
                    if cols is None:
                        dst = raw[:, i % 3].rearrange("p k c -> p (k c)").rearrange("p (m d) -> p m d", d=D)
                    else:
                        dst = raw[:, i % 3, :, cols]
                    sp.dma_start(dst, src).then_inc(raw_in[i % 3], 16)

            for i in range(3):
                fetch(i)
            residual(NB - 1, between={1: [3], 3: [4]})
            residual(NB, between={-1: [5, 6]})

            def load_mid(n, slot):
                sp.dma_start(x2[:, slot], mid_f[n]).then_inc(x2_in[slot], 16)

            for t in range(TT):
                sp.wait_ge(mid_out[t], 16 * NB)
            sp.wait_ge(p_ready, 4 * NB)
            sp.wait_ge(t_full, T_P2)
            load_mid(0, 0)
            load_mid(1, 1)
            for i in range(7, len(PARTS)):
                fetch(i)

            def store(n, slot):
                for t in range(TT):
                    sp.wait_ge(m_free, M_P2 + 4 * n + t + 1)
                    sp.dma_start(out_f[n, :, t, :], x2[:, slot, t, :]).then_inc(out_done[slot], 16)

            with sp.Fori(0, NB // 2 - 1) as i:
                for s in range(2):
                    store(2 * i + s, s)
                    sp.wait_ge(out_done[s], 64 * i + 64)
                    load_mid(2 * i + s + 2, s)
            for s in range(2):
                store(NB - 2 + s, s)
            for s in range(2):
                sp.wait_ge(out_done[s], 64 * (NB // 2))

        @block.gpsimd
        def _(pool):
            steps = [0]

            def step(ins):
                steps[0] += 1
                ins.then_inc(const_step, 1)
                pool.wait_ge(const_step, steps[0])

            def select(t, pattern, base, channel, fill, op):
                step(nc.gpsimd.affine_select(out=t, in_=t, compare_op=op, fill=fill, base=base,
                                             pattern=pattern, channel_multiplier=channel))

            nc.gpsimd.memset(half[:, :], -0.5).then_inc(half_ready, 1)
            step(nc.gpsimd.memset(ident[:, :], 0.0))
            select(ident[:, :], [[-1, P]], 0, 1, 1.0, ALU.not_equal)

            def normalise(n):
                pool.wait_ge(stats_ready, 4 * n + 4)
                pool.sem_inc(pool_passed, 1)
                nc.gpsimd.tensor_scalar(rstd[:, :], mv[:, :, 1], 1.0, EPS, ALU.mult, ALU.add).then_inc(var_eps, 1)
                nc.gpsimd.tensor_scalar(nmean[:, :], mv[:, :, 0], -1.0, 0.0, ALU.mult, ALU.add).then_inc(var_eps, 1)
                pool.wait_ge(var_eps, 2 * n + 2)
                nc.gpsimd.tensor_tensor(rstd[:, :], rstd[:, :], half[:, :], ALU.pow).then_inc(rstd_ready, 1)
                pool.wait_ge(rstd_ready, n + 1)
                pool.sem_inc(pool_passed, 1)
                for t in range(TT):
                    nc.gpsimd.tensor_scalar(x_ln[:, t, :], x_ln[:, t, :], nmean[:, t:t + 1], rstd[:, t:t + 1],
                                            ALU.add, ALU.mult).then_inc(x_normed, 1)

            def probabilities(n, t):
                pool.wait_ge(rden_ready, 4 * n + t + 1)
                nc.gpsimd.tensor_tensor(e[:, t % 2], e[:, t % 2],
                                        rden[:, t % 2, :].unsqueeze(2).to_broadcast([P, H, SK]),
                                        ALU.mult).then_inc(p_ready, 1)

            pool.wait_ge(half_ready, 1)
            normalise(0)

            step(nc.gpsimd.memset(k_mask[:, :, :], 1.0))
            select(k_mask[:, :, :], [[-HD, HG], [0, SK]], 0, 1, 0.0, ALU.is_ge)
            select(k_mask[:, :, :], [[HD, HG], [0, SK]], HD - 1, -1, 0.0, ALU.is_ge)
            step(nc.gpsimd.memset(v_mask[:, :, :, :], 1.0))
            for c in range(3):
                m = v_mask[:, c]
                select(m, [[-SK, HG], [0, HD]], CS[c], 1, 0.0, ALU.is_ge)
                select(m, [[SK, HG], [0, HD]], SK - 1 - CS[c], -1, 0.0, ALU.is_ge)
            select(v_mask[:, 2], [[0, HG], [0, HD]], -(2 * CH - CS[2]), 1, 0.0, ALU.is_ge)
            step(nc.gpsimd.memset(causal[:, :, :], 0.0))
            nc.gpsimd.affine_select(out=causal[:, :, :], in_=causal[:, :, :], compare_op=ALU.is_ge, fill=NEG, base=0,
                                    pattern=[[0, HG], [-1, SK]], channel_multiplier=1).then_inc(consts_ready, 1)

            probabilities(0, 0)
            normalise(1)
            for t in range(1, TT):
                probabilities(0, t)
            with pool.Fori(1, NB - 1) as n:
                probabilities(n, 0)
                normalise(n + 1)
                for t in range(1, TT):
                    probabilities(n, t)

            got = [0, 0, 0]

            def convert(i):
                srcs, dst = PARTS[i]
                got[i % 3] += 16 * len(srcs)
                pool.wait_ge(raw_in[i % 3], got[i % 3])
                src = raw[:, i % 3]
                if len(srcs) == 1:
                    src = src.rearrange("p k c -> p (k c)").rearrange("p (m d) -> p m d", d=D)
                nc.gpsimd.tensor_copy(dst, src).then_inc(raw_used, 1)

            pool.wait_ge(m_full, m_base(NB - 1))
            for t in range(TT):
                probabilities(NB - 1, t)
                convert(t)
            for i in range(TT, MH):
                convert(i)
            pool.wait_ge(m_full, M_LAST + 4)

            def rstd2(n):
                pool.wait_ge(stats2_ready, 4 * n + 4)
                pool.sem_inc(pool_passed, 1)
                nc.gpsimd.tensor_scalar(rstd[:, :], mv[:, :, 1], 1.0, EPS, ALU.mult, ALU.add).then_inc(var2_eps, 1)
                pool.wait_ge(var2_eps, n + 1)
                nc.gpsimd.tensor_tensor(rstd[:, :], rstd[:, :], half[:, :], ALU.pow).then_inc(rstd2_ready, 1)

            def h_low(n, m):
                pool.wait_ge(h_hi, MH * n + m + 1)
                nc.gpsimd.tensor_tensor(hT[:, 1, m, :], hid[:, m % 2, :], hT[:, 0, m, :].bitcast(f32),
                                        ALU.subtract).then_inc(h_lo, 1)

            rstd2(0)
            left = list(range(MH, len(PARTS)))
            for m in range(MH):
                h_low(0, m)
                if left:
                    convert(left.pop(0))
                if m == 6:
                    rstd2(1)
            with pool.Fori(1, NB - 1) as n:
                for m in range(MH):
                    h_low(n, m)
                    if m == 6:
                        rstd2(n + 1)
            for m in range(MH):
                h_low(NB - 1, m)

        @block.scalar
        def _(act):
            act.dma_start(gates[:, 0:1], g_xattn).then_inc(gates_in, 16)
            act.dma_start(gates[:, 1:2], g_ffn).then_inc(gates_in, 16)
            act.wait_ge(gates_in, 32)
            nc.scalar.activation(gate_t[:, :], gates[:, :], ACT.Tanh).then_inc(gates_tanh, 1)

            def split_hi(n_arrived, arrived, dst, src):
                act.wait_ge(arrived, n_arrived)
                nc.scalar.activation(dst, src, ACT.Copy).then_inc(w_hi, 1)

            split_hi(16, wq_in, wq[:, 0], wq_stage[:, :, :])

            def kv_high(i, dst, src):
                act.wait_ge(kv_full, i + 1)
                nc.scalar.activation(dst, src, ACT.Copy).then_inc(kv_hi, 1)

            def t_high(i, slot, dst, src_rows=P):
                act.wait_ge(t_full, i + 1)
                src = t_bank[slot % 2][0:src_rows, :].rearrange("p (c n) -> p c n", c=4)
                nc.scalar.activation(dst, src, ACT.Copy).then_inc(t_hi, 1)

            def x_high(i, t, dst=None):
                t_high(i, t, (xT if dst is None else dst)[:, 0, :, t * P:(t + 1) * P])

            def p_high(n, t, r, at):
                t_high(t_base(n) + at, at, pT[0:CH, 0, 4 * r:4 * r + 4, t * P:(t + 1) * P], CH)

            def m_high(i, slot, dst):
                act.wait_ge(m_full, i + 1)
                nc.scalar.activation(dst, m_bank[slot % 2][:, :], ACT.Copy).then_inc(m_hi, 1)

            def exp0(n, t):
                act.wait_ge(s0_shifted, 4 * n + t + 1)
                nc.scalar.activation(e[:, t % 2, 0:UH, :], e[:, t % 2, 0:UH, :], ACT.Exp, scale=SCALE)\
                    .then_inc(exp0_done, 1)

            def exp1(n, t):
                act.wait_ge(nmx_ready, 4 * n + t + 1)
                for h in range(UH):
                    last = nc.scalar.activation(
                        e[:, t % 2, UH + h, :], s_bank[1][:, h // HG, (h % HG) * SK:(h % HG + 1) * SK], ACT.Exp,
                        bias=nmx[:, t % 2, h:h + 1], scale=SCALE, accum_out=den[:, t % 2, UH + h:UH + h + 1])
                last.then_inc(exp1_done, 1)

            for t in range(TT):
                x_high(t, t)
            for m in range(G):
                for b in range(B):
                    i = B * m + b
                    kv_high(i, K[:, 0, b, m, :], k_full[:, i % 2].rearrange("p h k -> p (h k)"))
            for m in range(G):
                m_high(4 + m, m, qT[:, 0, m, :])
            split_hi(16, wo_in, wo[:, 0], wo_stage[:, :, :])

            def step(n, values, query):
                exp0(n, 0)
                if values == "first":
                    for c in range(3 * B):
                        kv_high(G * B + c, V[0:CH, 0, c // 3, :, :].rearrange("p (m c) n -> p m c n", c=3)[:, :, c % 3, :],
                                v_full[0:CH, c % 2])
                    exp1(n, 0)
                else:
                    m_high(m_base(n), 0, aT[:, 0, 0, :])
                    exp1(n, 0)
                    for m in range(1, G):
                        m_high(m_base(n) + m, m, aT[:, 0, m, :])
                for t in (1, 2):
                    exp0(n, t)
                    p_high(n, t - 1, 0, 3 * t - 3)
                    exp1(n, t)
                    p_high(n, t - 1, 1, 3 * t - 2)
                    p_high(n, t - 1, 2, 3 * t - 1)
                at = 6
                if query:
                    for t in range(3):
                        x_high(t_base(n) + 6 + t, t)
                exp0(n, 3)
                if query:
                    x_high(t_base(n) + 9, 3)
                    at = 10
                exp1(n, 3)
                q_at = (m_base(n) + 8) if values != "first" else M_Q1
                p_high(n, 2, 0, at)
                if query:
                    m_high(q_at, 0, qT[:, 0, 0, :])
                p_high(n, 2, 1, at + 1)
                if query:
                    m_high(q_at + 1, 1, qT[:, 0, 1, :])
                p_high(n, 2, 2, at + 2)
                if query:
                    m_high(q_at + 2, 2, qT[:, 0, 2, :])
                p_high(n, 3, 0, at + 3)
                p_high(n, 3, 1, at + 4)
                if query:
                    m_high(q_at + 3, 3, qT[:, 0, 3, :])
                p_high(n, 3, 2, at + 5)

            step(0, "first", True)
            with act.Fori(1, NB - 1) as n:
                step(n, "loop", True)
            step(NB - 1, "loop", False)
            for m in range(G):
                m_high(M_LAST + m, m, aT[:, 0, m, :])

            for t in range(TT):
                x_high(T_P2 + t, t, xT2)

            def tanh_gate(n, m):
                act.wait_ge(gu_full, MH * n + m + 1)
                nc.scalar.activation(th[:, m % 2, :], psum[:, 2 * (m % 2), :], ACT.Tanh, scale=0.5 * W_SCALE)\
                    .then_inc(tanh_done, 1)

            def h_high(n, m):
                act.wait_ge(gu_free, MH * n + m + 1)
                nc.scalar.activation(hT[:, 0, m, :], hid[:, m % 2, :], ACT.Copy).then_inc(h_hi, 1)

            def ffn(n, more):
                tanh_gate(n, 0)
                for m in range(MH):
                    if m + 1 < MH:
                        tanh_gate(n, m + 1)
                    h_high(n, m)
                if more:
                    for t in range(TT):
                        x_high(T_P2 + 4 * n + 4 + t, t, xT2)

            ffn(0, True)
            with act.Fori(1, NB - 1) as n:
                ffn(n, True)
            ffn(NB - 1, False)

        @block.vector
        def _(dve):
            def stats(n, t):
                dve.wait_ge(x_in, 16 * n + 16) if t == 0 else None
                nc.vector.bn_stats(bn[:, t, :], x_ln[:, t, :]).then_inc(bn_done, 1)
                dve.wait_ge(bn_done, 4 * n + t + 1)
                dve.sem_inc(dve_passed, 1)
                nc.vector.bn_aggr(mv[:, t, :], bn[:, t, :]).then_inc(stats_ready, 1)

            def split_lo(i, dst, src, hi):
                dve.wait_ge(w_hi, i)
                nc.vector.tensor_tensor(dst, src, hi.bitcast(f32), ALU.subtract).then_inc(w_split, 1)

            def t_low(i, slot, dst, hi, rows=P):
                dve.wait_ge(t_hi, i + 1)
                src = t_bank[slot % 2][0:rows, :].rearrange("p (c n) -> p c n", c=4)
                nc.vector.tensor_tensor(dst, src, hi.bitcast(f32), ALU.subtract).then_inc(t_free, 1)

            def x_low(i, t, of=None):
                of = xT if of is None else of
                c = slice(t * P, (t + 1) * P)
                t_low(i, t, of[:, 1, :, c], of[:, 0, :, c])

            def p_low(n, t, r, at):
                c = slice(t * P, (t + 1) * P)
                rr = slice(4 * r, 4 * r + 4)
                t_low(t_base(n) + at, at, pT[0:CH, 1, rr, c], pT[0:CH, 0, rr, c], CH)

            def m_low(hi_count, slot, dst, hi):
                dve.wait_ge(m_hi, hi_count)
                nc.vector.tensor_tensor(dst, m_bank[slot % 2][:, :], hi.bitcast(f32), ALU.subtract)\
                    .then_inc(m_free, 1)

            def v_low(n, m):
                m_low(h_base(n) + m + 1, m, aT[:, 1, m, :], aT[:, 0, m, :])

            def q_low(hi_count, m):
                m_low(hi_count, m, qT[:, 1, m, :], qT[:, 0, m, :])

            def unit(u):
                return s_bank[u][:, :, 0:GK].rearrange("p g (h k) -> p g h k", h=HG)

            def shift(n, t):
                dve.wait_ge(s0_full, 4 * n + t + 1)
                nc.vector.reduce_max(mx[:, t % 2, 0:UH], unit(0), AX.X).then_inc(mx0_done, 1)
                dve.wait_ge(mx0_done, 4 * n + t + 1)
                for g in range(2):
                    last = nc.vector.tensor_tensor(
                        e[:, t % 2, g * HG:(g + 1) * HG, :], unit(0)[:, g],
                        mx[:, t % 2, g * HG:(g + 1) * HG].unsqueeze(2).to_broadcast([P, HG, SK]), ALU.subtract)
                last.then_inc(s0_shifted, 1)
                dve.wait_ge(s1_full, 4 * n + t + 1)
                nc.vector.reduce_max(mx[:, t % 2, UH:H], unit(1), AX.X).then_inc(mx1_done, 1)
                dve.wait_ge(mx1_done, 4 * n + t + 1)
                nc.vector.tensor_scalar(nmx[:, t % 2, :], mx[:, t % 2, UH:H], -SCALE, None, ALU.mult)\
                    .then_inc(nmx_ready, 1)

            def slot_free(n, t, query):
                if t >= 2:
                    dve.wait_ge(t_full, t_base(n) + 3 * (t - 1))
                else:
                    dve.wait_ge(t_full, t_base(n) - 3 + 3 * t)

            def denominators(n, t):
                dve.wait_ge(exp0_done, 4 * n + t + 1)
                nc.vector.reduce_sum(den[:, t % 2, 0:UH], e[:, t % 2, 0:UH, :], AX.X).then_inc(sum_done, 1)
                dve.wait_ge(sum_done, 4 * n + t + 1)
                dve.wait_ge(exp1_done, 4 * n + t + 1)
                nc.vector.reciprocal(rden[:, t % 2, :], den[:, t % 2, :]).then_inc(rden_ready, 1)

            def residual(n, t):
                dve.wait_ge(m_full, m_base(n) + 5 + t)
                dve.wait_ge(res_in[t], 16 * n)
                nc.vector.scalar_tensor_tensor(x_res[:, t, :], m_bank[t % 2][:, :], gate_t[:, 0:1], x_res[:, t, :],
                                               ALU.mult, ALU.add).then_inc(m_free, 1)

            for t in range(TT):
                stats(0, t)
            split_lo(1, wq[:, 1], wq_stage[:, :, :], wq[:, 0])
            for t in range(TT):
                x_low(t, t)
            dve.wait_ge(const_step, 5)
            for m in range(G):
                dve.wait_ge(m_full, m + 1)
                for b in range(B):
                    i = B * m + b
                    full = k_full[:, i % 2]
                    nc.vector.tensor_tensor(
                        full, m_bank[m % 2][:, b * SK:(b + 1) * SK].unsqueeze(1).to_broadcast([P, HG, SK]),
                        k_mask[:, :, :], ALU.mult).then_inc(kv_full, 1)
                    dve.wait_ge(kv_full, i + 1)
                    dve.wait_ge(kv_hi, i + 1)
                    low = nc.vector.tensor_tensor(K[:, 1, b, m, :], full.rearrange("p h k -> p (h k)"),
                                                  K[:, 0, b, m, :].bitcast(f32), ALU.subtract)
                low.then_inc(m_free, 1)
            for m in range(G):
                q_low(m + 1, m)
            split_lo(2, wo[:, 1], wo_stage[:, :, :], wo[:, 0])
            dve.wait_ge(gates_tanh, 1)
            nc.vector.tensor_scalar(gate_ffn[:, :], gate_t[:, 1:2], 0.5 * W_SCALE ** 3, None, ALU.mult)\
                .then_inc(gate_ready, 1)

            def step(n, values, query):
                slot = (lambda t: None) if values == "first" else (lambda t: slot_free(n, t, query))
                slot(0)
                shift(n, 0)
                if values == "first":
                    dve.wait_ge(consts_ready, 1)
                    for c in range(3 * B):
                        full = v_full[0:CH, c % 2]
                        i = G * B + c
                        dve.wait_ge(m_full, V_AT + c + 1)
                        nc.vector.tensor_tensor(
                            full, m_bank[c % 2][0:CH, :].rearrange("p (m n) -> p m n", m=G),
                            v_mask[0:CH, c % 3].rearrange("p h d -> p (h d)").unsqueeze(1).to_broadcast([CH, G, P]),
                            ALU.mult).then_inc(kv_full, 1)
                        dve.wait_ge(kv_full, i + 1)
                        dve.wait_ge(kv_hi, i + 1)
                        lo, hi = (V[0:CH, q, c // 3].rearrange("p (m c) n -> p m c n", c=3)[:, :, c % 3, :]
                                  for q in (1, 0))
                        nc.vector.tensor_tensor(lo, full, hi.bitcast(f32), ALU.subtract).then_inc(m_free, 1)
                    for t in range(TT):
                        stats(n + 1, t)
                    denominators(n, 0)
                else:
                    for m in range(G):
                        v_low(n, m)
                        if query:
                            stats(n + 1, m)
                        if m == 1:
                            denominators(n, 0)
                slot(1)
                shift(n, 1)
                p_low(n, 0, 0, 0)
                p_low(n, 0, 1, 1)
                if values != "first":
                    residual(n, 0)
                p_low(n, 0, 2, 2)
                denominators(n, 1)
                if values != "first":
                    residual(n, 1)
                slot_free(n, 2, query)
                shift(n, 2)
                p_low(n, 1, 0, 3)
                p_low(n, 1, 1, 4)
                if values != "first":
                    residual(n, 2)
                p_low(n, 1, 2, 5)
                if query:
                    x_low(t_base(n) + 6, 0)
                denominators(n, 2)
                if values != "first":
                    residual(n, 3)
                at = 6
                if query:
                    x_low(t_base(n) + 7, 1)
                    x_low(t_base(n) + 8, 2)
                    at = 10
                slot_free(n, 3, query)
                shift(n, 3)
                if query:
                    x_low(t_base(n) + 9, 3)
                q_at = (h_base(n) + 5) if values != "first" else 5
                p_low(n, 2, 0, at)
                if query:
                    q_low(q_at, 0)
                p_low(n, 2, 1, at + 1)
                denominators(n, 3)
                if query:
                    q_low(q_at + 1, 1)
                p_low(n, 2, 2, at + 2)
                if query:
                    q_low(q_at + 2, 2)
                p_low(n, 3, 0, at + 3)
                p_low(n, 3, 1, at + 4)
                if query:
                    q_low(q_at + 3, 3)
                p_low(n, 3, 2, at + 5)

            step(0, "first", True)
            with dve.Fori(1, NB - 1) as n:
                step(n, "loop", True)
            step(NB - 1, "loop", False)
            for m in range(G):
                m_low(H_LAST + m + 1, m, aT[:, 1, m, :], aT[:, 0, m, :])
            for t in range(TT):
                residual(NB, t)

            def stats2(n, slot, t, arrived):
                if t == 0:
                    dve.wait_ge(x2_in[slot], arrived)
                nc.vector.bn_stats(bn[:, t, :], x2[:, slot, t, :]).then_inc(bn2_done, 1)
                dve.wait_ge(bn2_done, 4 * n + t + 1)
                dve.sem_inc(dve_passed, 1)
                nc.vector.bn_aggr(mv[:, t, :], bn[:, t, :]).then_inc(stats2_ready, 1)

            def normalise2(n, slot):
                dve.wait_ge(rstd2_ready, n + 1)
                for t in range(TT):
                    nc.vector.tensor_scalar(xh[:, t, :], x2[:, slot, t, :], mv[:, t, 0:1], rstd[:, t:t + 1],
                                            ALU.subtract, ALU.mult).then_inc(x2_normed, 1)

            def hidden(n, m):
                dve.wait_ge(tanh_done, MH * n + m + 1)
                nc.vector.scalar_tensor_tensor(th[:, m % 2, :], th[:, m % 2, :], 1.0, psum[:, 2 * (m % 2), :],
                                               ALU.add, ALU.mult).then_inc(silu_done, 1)
                dve.wait_ge(silu_done, MH * n + m + 1)
                if m < 2:
                    if not (isinstance(n, int) and n == 0):
                        dve.wait_ge(h_lo, MH * n + m - 1)
                else:
                    dve.wait_ge(h_lo, MH * n + m - 1)
                nc.vector.tensor_tensor(hid[:, m % 2, :], th[:, m % 2, :], psum[:, 2 * (m % 2) + 1, :], ALU.mult)\
                    .then_inc(gu_free, 1)

            def result(n, slot):
                for t in range(TT):
                    dve.wait_ge(m_full, M_P2 + 4 * n + t + 1)
                    nc.vector.scalar_tensor_tensor(x2[:, slot, t, :], m_bank[t % 2][:, :], gate_ffn[:, 0:1],
                                                   x2[:, slot, t, :], ALU.mult, ALU.add).then_inc(m_free, 1)

            def ffn(n, slot, arrived, more):
                for m in range(MH):
                    hidden(n, m)
                    if more and 2 <= m < 2 + TT:
                        stats2(n + 1, 1 - slot, m - 2, arrived)
                    if more and m == 8:
                        normalise2(n + 1, 1 - slot)
                if more:
                    for t in range(TT):
                        x_low(T_P2 + 4 * n + 4 + t, t, xT2)
                result(n, slot)

            for t in range(TT):
                stats2(0, 0, t, 16)
            normalise2(0, 0)
            for t in range(TT):
                x_low(T_P2 + t, t, xT2)
            dve.wait_ge(gate_ready, 1)
            ffn(0, 0, 16, True)
            with dve.Fori(0, NB // 2 - 1) as i:
                ffn(2 * i + 1, 1, 16 * i + 32, True)
                ffn(2 * i + 2, 0, 16 * i + 32, True)
            ffn(NB - 1, 1, 0, False)

        @block.tensor
        def _(pe):
            def product(dst, terms):
                for j, (stat, mov) in enumerate(terms):
                    last = nc.tensor.matmul(dst, stat, mov, start=(j == 0), stop=(j == len(terms) - 1))
                return last

            CROSS = ((0, 0), (1, 0), (0, 1))

            def t_wait(i, always=False):
                if always or not (isinstance(i, int) and i < 2):
                    pe.wait_ge(t_free, i - 1)

            def m_wait(i):
                if not (isinstance(i, int) and i < 2):
                    pe.wait_ge(m_free, i - 1)

            def transpose_x(i, t, normed, ready, src):
                pe.wait_ge(ready, normed)
                t_wait(i)
                for k in range(KD):
                    last = nc.tensor.transpose(t_bank[t % 2][:, k * P:(k + 1) * P], src[:, t, k * P:(k + 1) * P],
                                               ident[:, :])
                last.then_inc(t_full, 1)

            def transpose_p(n, t, r, at):
                if r == 0:
                    pe.wait_ge(p_ready, 4 * n + t + 1)
                t_wait(t_base(n) + at)
                rows = e[:, t % 2].rearrange("p h k -> p (h k)")
                for j in range(4):
                    g, c = divmod(4 * r + j, 3)
                    last = nc.tensor.transpose(t_bank[at % 2][0:CH, j * P:(j + 1) * P],
                                               rows[:, g * GK + CS[c]:g * GK + CS[c] + CH], ident[:, :])
                last.then_inc(t_full, 1)

            def query(i, m):
                m_wait(i)
                product(m_bank[m % 2][:, :],
                        [(wq[:, a, k, m * P:(m + 1) * P], xT[:, c, k, :]) for k in range(KD) for a, c in CROSS]
                        ).then_inc(m_full, 1)

            def scores(n, t, b, masked):
                for u in range(2):
                    if not (isinstance(n, int) and n == 0 and t == 0):
                        pe.wait_ge((s0_shifted, exp1_done)[u], 4 * n + t)
                    for g in range(2):
                        m = 2 * u + g
                        terms = [(qT[:, a, m, t * P:(t + 1) * P], K[:, c, b, m, :]) for a, c in CROSS]
                        if masked:
                            terms.append((ident[:, :], causal[:, :, :].rearrange("p h k -> p (h k)")))
                        last = product(s_bank[u][:, g, 0:GK], terms)
                    last.then_inc((s0_full, s1_full)[u], 1)

            def values(i, m, b, split):
                pe.wait_ge(t_free, split)
                m_wait(i)
                product(m_bank[m % 2][:, :],
                        [(V[0:CH, a, b, 3 * m + c, :], pT[0:CH, d, 3 * m + c, :]) for c in range(3) for a, d in CROSS]
                        ).then_inc(m_full, 1)

            def project(i, t):
                m_wait(i)
                product(m_bank[t % 2][:, :],
                        [(aT[:, a, m, t * P:(t + 1) * P], wo[:, c, m, :]) for m in range(G) for a, c in CROSS]
                        ).then_inc(m_full, 1)

            pe.wait_ge(const_step, 2)
            for t in range(TT):
                transpose_x(t, t, t + 1, x_normed, x_ln)
            pe.wait_ge(ctx_in, 16)
            pe.wait_ge(wk_in, 16)
            for m in range(G):
                m_wait(m)
                product(m_bank[m % 2][:, 0:B * SK],
                        [(wk_stage[:, k, m * P:(m + 1) * P], ctx_stage[:, k, :]) for k in range(KD)]
                        ).then_inc(m_full, 1)
            pe.wait_ge(w_split, 1)
            pe.wait_ge(t_free, 4)
            for m in range(G):
                query(4 + m, m)
            pe.wait_ge(consts_ready, 1)

            def step(n, b, b_before, masked, first, more):
                base = None if first else m_base(n)
                q_at = M_Q1 if first else base + 8
                pe.wait_ge(m_free, 8 if first else (m_base(n)))
                scores(n, 0, b, masked)
                if first:
                    pe.wait_ge(wv_in, 16)
                    pe.wait_ge(rep_in, 16 * HG * B)
                    for c in range(3 * B):
                        m_wait(V_AT + c)
                        product(m_bank[c % 2][0:CH, :],
                                [(ctx_rep[:, k, c // 3, CS[c % 3]:CS[c % 3] + CH], wv_stage[:, k, :])
                                 for k in range(KD)]).then_inc(m_full, 1)
                    pe.wait_ge(w_split, 2)
                else:
                    for m in range(G):
                        values(base + m, m, b_before, t_base(n) - 2 + min(m, 2))
                scores(n, 1, b, False)
                transpose_p(n, 0, 0, 0)
                transpose_p(n, 0, 1, 1)
                if not first:
                    pe.wait_ge(m_free, base + 4)
                    project(base + 4, 0)
                transpose_p(n, 0, 2, 2)
                if not first:
                    project(base + 5, 1)
                scores(n, 2, b, False)
                transpose_p(n, 1, 0, 3)
                transpose_p(n, 1, 1, 4)
                if not first:
                    project(base + 6, 2)
                transpose_p(n, 1, 2, 5)
                at = 6
                if more:
                    transpose_x(t_base(n) + 6, 0, 4 * n + 5, x_normed, x_ln)
                if not first:
                    project(base + 7, 3)
                if more:
                    transpose_x(t_base(n) + 7, 1, 4 * n + 6, x_normed, x_ln)
                    transpose_x(t_base(n) + 8, 2, 4 * n + 7, x_normed, x_ln)
                scores(n, 3, b, False)
                if more:
                    transpose_x(t_base(n) + 9, 3, 4 * n + 8, x_normed, x_ln)
                    at = 10
                transpose_p(n, 2, 0, at)
                if more:
                    pe.wait_ge(t_free, t_base(n) + 10)
                    query(q_at, 0)
                transpose_p(n, 2, 1, at + 1)
                if more:
                    query(q_at + 1, 1)
                transpose_p(n, 2, 2, at + 2)
                if more:
                    query(q_at + 2, 2)
                transpose_p(n, 3, 0, at + 3)
                transpose_p(n, 3, 1, at + 4)
                if more:
                    query(q_at + 3, 3)
                transpose_p(n, 3, 2, at + 5)

            step(0, 0, 0, True, True, True)
            for b in range(B):
                if b:
                    step(b * BPB, b, b - 1, True, False, True)
                with pe.Fori(b * BPB + 1, (b + 1) * BPB - (b == B - 1)) as n:
                    step(n, b, b, False, False, True)
            step(NB - 1, B - 1, B - 1, False, False, False)
            for m in range(G):
                values(M_LAST + m, m, B - 1, T_P2 - 2 + min(m, 2))
            pe.wait_ge(m_free, M_LAST + 4)
            for t in range(TT):
                project(M_LAST + 4 + t, t)

            def gate_up(n, m, weights=None):
                if m < 2:
                    if not (isinstance(n, int) and n == 0):
                        pe.wait_ge(gu_free, MH * n + m - 1)
                else:
                    pe.wait_ge(gu_free, MH * n + m - 1)
                if weights is not None:
                    pe.wait_ge(raw_used, weights)
                for j in range(2):
                    c = (2 * m + j) * P
                    last = product(psum[:, 2 * (m % 2) + j, :],
                                   [(w_gu[:, k, c:c + P], xT2[:, a, k, :]) for k in range(KD) for a in range(2)])
                last.then_inc(gu_full, 1)

            def down(n, t):
                m_wait(M_P2 + 4 * n + t)
                terms = [(hT[:, a, m, t * P:(t + 1) * P], w_d[:, m, :]) for m in range(MH) for a in range(2)]
                for j, (stat, mov) in enumerate(terms):
                    if t == 0 and j % 2 == 0:
                        pe.wait_ge(h_lo, MH * n + j // 2 + 1)
                    last = nc.tensor.matmul(m_bank[t % 2][:, :], stat, mov, start=(j == 0), stop=(j == len(terms) - 1))
                last.then_inc(m_full, 1)

            def ffn(n, more, first=False):
                pe.wait_ge(t_free, T_P2 + 4 * n + 4)
                for m in range(MH):
                    gate_up(n, m, m + 1 if first else None)
                if more:
                    for t in range(TT):
                        transpose_x(T_P2 + 4 * n + 4 + t, t, 4 * n + 5 + t, x2_normed, xh)
                if first:
                    pe.wait_ge(raw_used, len(PARTS))
                for t in range(TT):
                    down(n, t)

            for t in range(TT):
                transpose_x(T_P2 + t, t, t + 1, x2_normed, xh)
            ffn(0, True, True)
            with pe.Fori(1, NB - 1) as n:
                ffn(n, True)
            ffn(NB - 1, False)


def kernel(**inputs):
    import numpy as np
    import concourse.bacc as bacc
    from concourse.bass_utils import run_bass_kernel_spmd as run

    def t(name):
        return np.ascontiguousarray(np.asarray(inputs[name]).T)

    c = np.asarray(inputs["ctx_1024"])
    x = np.ascontiguousarray(inputs["x"])
    arrays = {
        "x": x,
        "ctx_t": np.ascontiguousarray(c.reshape(-1, c.shape[2]).T),
        "g_xattn": np.ascontiguousarray(np.broadcast_to(np.asarray(inputs["g_xattn"]).reshape(1, 1), (128, 1))),
        "g_ffn": np.ascontiguousarray(np.broadcast_to(np.asarray(inputs["g_ffn"]).reshape(1, 1), (128, 1))),
        "wq_t": t("L0_xattn_Wq"), "wk_t": t("L0_xattn_Wk"), "wv_t": t("L0_xattn_Wv"), "wo_t": t("L0_xattn_Wo"),
        "w_gate_t": t("L0_ffn_w_gate"), "w_up_t": t("L0_ffn_w_up"), "w_down_t": t("L0_ffn_w_down"),
    }
    nc = bacc.Bacc("TRN2", target_bir_lowering=False, num_devices=1,
                   dynamic_dma_scratch_size=1024)
    args = [nc.dram_tensor(n, a.shape, mybir.dt.from_np(a.dtype), kind="ExternalInput").ap() for n, a in arrays.items()]
    args.append(nc.dram_tensor("x_mid", (x.shape[0] * x.shape[1], x.shape[2]), mybir.dt.float32, kind="Internal").ap())
    args.append(nc.dram_tensor("out", x.shape, mybir.dt.float32, kind="ExternalOutput").ap())
    flamingo_gated_block(nc, *args)
    r = run(nc, [arrays], core_ids=[0])
    return r.results[0]["out"]
```

```python
import concourse.bass as bass
from concourse import mybir
from contextlib import ExitStack


def flamingo_gated_block(
    nc: bass.Bass,
    x: bass.AP,
    ctx_t: bass.AP,
    g_xattn: bass.AP,
    g_ffn: bass.AP,
    wq_t: bass.AP,
    wk_t: bass.AP,
    wv_t: bass.AP,
    wo_t: bass.AP,
    w_gate_t: bass.AP,
    w_up_t: bass.AP,
    w_down_t: bass.AP,
    x_mid: bass.AP,
    out: bass.AP,
):
    f32, f32r, i32 = mybir.dt.float32, mybir.dt.float32r, mybir.dt.int32
    ALU = mybir.AluOpType
    ACT = mybir.ActivationFunctionType
    AX = mybir.AxisListType

    P = 128
    B, SQ, D = x.shape
    SK = ctx_t.shape[1] // B
    HID = w_gate_t.shape[1]
    H, HD = 16, 32
    SCALE = HD ** -0.5
    NEG = -1e9
    EPS = 1e-5
    W_SCALE = 1.0 / 127.0
    KD = D // P
    TT = 4
    TB = TT * P
    NB = B * SQ // TB
    BPB = SQ // TB
    HG = P // HD
    G = H // HG
    GK = HG * SK
    UH = H // 2
    CH = -(-GK // 3)
    CS = [0, CH, GK - CH]
    NC = 3 * G
    MH = HID // P

    x_f = x.rearrange("b s d -> (b s) d").rearrange("(n t p) d -> n p t d", p=P, t=TT)
    out_f = out.rearrange("b s d -> (b s) d").rearrange("(n t p) d -> n p t d", p=P, t=TT)
    mid_f = x_mid.rearrange("(n t p) d -> n p t d", p=P, t=TT)

    def t_base(n):
        return 4 + 16 * n

    V_AT = 4 + 4
    M_Q1 = V_AT + 6

    def m_base(n):
        return M_Q1 + 4 + 12 * (n - 1) - (4 if isinstance(n, int) and n == NB else 0)

    def h_base(n):
        return 8 + 8 * (n - 1)

    T_P2 = t_base(NB - 1) + 12
    M_LAST = m_base(NB)
    M_P2 = M_LAST + 8
    H_LAST = h_base(NB - 1) + 4

    ctx = ExitStack()
    with ctx:
        def sb(name, shape, dt=f32, where=ctx):
            return where.enter_context(nc.sbuf_tensor(name, shape, dt))

        def sem(name):
            return ctx.enter_context(nc.semaphore(name))

        ident = sb("ident", [P, P])
        causal = sb("causal", [P, HG, SK])
        gates = sb("gates", [P, 2])
        gate_t = sb("gate_t", [P, 2])
        gate_ffn = sb("gate_ffn", [P, 1])
        bn = sb("bn", [P, TT, 6])
        mv = sb("mv", [P, TT, 2])
        rstd = sb("rstd", [P, TT])
        nmean = sb("nmean", [P, TT])
        half = sb("half", [P, TT])
        mx = sb("mx", [P, 2, H])
        nmx = sb("nmx", [P, 2, UH])
        den = sb("den", [P, 2, H])
        rden = sb("rden", [P, 2, H])
        raw = sb("raw", [P, 3, KD, P * 2], i32)

        with ExitStack() as a1:
            wq = sb("wq", [P, 2, KD, D], f32r, a1)
            xT = sb("xT", [P, 2, KD, TB], f32r, a1)
            x_ln = sb("x_ln", [P, TT, D], f32, a1)
            wv_stage = sb("wv_stage", [P, KD, D], f32, a1)
        w_gu = sb("w_gu", [P, KD, 2 * HID], f32r)
        with ExitStack() as b1:
            qT = sb("qT", [P, 2, G, TB], f32r, b1)
            K = sb("K", [P, 2, B, G, GK], f32r, b1)
            e = sb("e", [P, 2, H, SK], f32, b1)
        with ExitStack() as b2:
            x2 = sb("x2", [P, 2, TT, D], f32, b2)
            xh = sb("xh", [P, TT, D], f32, b2)
            xT2 = sb("xT2", [P, 2, KD, TB], f32r, b2)
        sb("region_b", [P, 2 * G * TB + 2 * B * G * GK + 2 * H * SK])
        with ExitStack() as c0:
            wq_stage = sb("wq_stage", [P, KD, D], f32, c0)
            wk_stage = sb("wk_stage", [P, KD, D], f32, c0)
            wo_stage = sb("wo_stage", [P, KD, D], f32, c0)
            ctx_stage = sb("ctx_stage", [P, KD, B * SK], f32, c0)
            k_mask = sb("k_mask", [P, HG, SK], f32, c0)
            k_full = sb("k_full", [P, 2, HG, SK], f32, c0)
        with ExitStack() as c1:
            pT = sb("pT", [P, 2, NC, TB], f32r, c1)
        hT = sb("hT", [P, 2, MH, TB], f32r)
        with ExitStack() as d1:
            V = sb("V", [P, 2, B, NC, P], f32r, d1)
        w_d = sb("w_d", [P, MH, D], f32r)
        with ExitStack() as e0:
            ctx_rep = sb("ctx_rep", [P, KD, B, GK], f32, e0)
            v_mask = sb("v_mask", [P, 3, HG, HD], f32, e0)
            v_full = sb("v_full", [P, 2, G, P], f32, e0)
        with ExitStack() as e2:
            th = sb("th", [P, 2, TB], f32, e2)
            hid = sb("hid", [P, 2, TB], f32, e2)
        aT = sb("aT", [P, 2, G, TB], f32r)
        wo = sb("wo", [P, 2, KD, D], f32r)
        x_res = sb("x_res", [P, TT, D])

        psum = ctx.enter_context(nc.psum_tensor("psum", [P, 8, 512], f32))
        s_bank = [psum[:, 0:2, :], psum[:, 2:4, :]]
        t_bank = [psum[:, 4, :], psum[:, 5, :]]
        m_bank = [psum[:, 6, :], psum[:, 7, :]]

        consts_ready = sem("consts_ready")
        const_step = sem("const_step")
        half_ready = sem("half_ready")
        gates_in = sem("gates_in")
        gates_tanh = sem("gates_tanh")
        gate_ready = sem("gate_ready")
        wq_in, wk_in, wv_in, wo_in = sem("wq_in"), sem("wk_in"), sem("wv_in"), sem("wo_in")
        ctx_in, rep_in = sem("ctx_in"), sem("rep_in")
        w_hi = sem("w_hi")
        w_split = sem("w_split")
        kv_full = sem("kv_full")
        kv_hi = sem("kv_hi")
        x_in = [sem(f"x_in{t}") for t in range(TT)]
        bn_done = sem("bn_done")
        stats_ready = sem("stats_ready")
        var_eps = sem("var_eps")
        rstd_ready = sem("rstd_ready")
        x_normed = sem("x_normed")
        dve_passed, pool_passed = sem("dve_passed"), sem("pool_passed")
        t_full, t_hi, t_free = sem("t_full"), sem("t_hi"), sem("t_free")
        m_full, m_hi, m_free = sem("m_full"), sem("m_hi"), sem("m_free")
        s0_full, s1_full = sem("s0_full"), sem("s1_full")
        mx0_done, mx1_done = sem("mx0_done"), sem("mx1_done")
        s0_shifted = sem("s0_shifted")
        nmx_ready = sem("nmx_ready")
        exp0_done, exp1_done = sem("exp0_done"), sem("exp1_done")
        sum_done = sem("sum_done")
        rden0_ready, rden1_ready = sem("rden0_ready"), sem("rden1_ready")
        p0_ready, p1_ready = sem("p0_ready"), sem("p1_ready")
        res_in = [sem(f"res_in{t}") for t in range(TT)]
        mid_out = [sem(f"mid_out{t}") for t in range(TT)]
        raw_in = [sem(f"raw_in{i}") for i in range(3)]
        raw_used = sem("raw_used")
        x2_in = [sem(f"x2_in{i}") for i in range(2)]
        bn2_done, stats2_ready = sem("bn2_done"), sem("stats2_ready")
        var2_eps, rstd2_ready = sem("var2_eps"), sem("rstd2_ready")
        x2_normed = sem("x2_normed")
        gu_full, tanh_done, gu_free = sem("gu_full"), sem("tanh_done"), sem("gu_free")
        silu_done = sem("silu_done")
        h_hi, h_lo = sem("h_hi"), sem("h_lo")
        out_done = [sem(f"out_done{i}") for i in range(2)]

        def raw_parts():
            gate = w_gate_t.rearrange("(k p) h -> p k h", p=P)
            up = w_up_t.rearrange("(k p) h -> p k h", p=P)
            down = w_down_t.rearrange("(k p) d -> p k d", p=P)
            parts = []
            for m in range(MH):
                c = slice(m * P, (m + 1) * P)
                parts.append(([(gate[:, :, c], slice(0, P)), (up[:, :, c], slice(P, 2 * P))],
                              w_gu[:, :, 2 * P * m:2 * P * (m + 1)]))
            for m in range(0, MH, 2):
                parts.append(([(down[:, m:m + 2, :], None)], w_d[:, m:m + 2, :]))
            return parts

        PARTS = raw_parts()

        block = ctx.enter_context(nc.Block())

        @block.sync
        def _(sp):
            def load_x(n, first=False):
                if not first:
                    sp.wait_ge(t_full, t_base(n - 2) + 4)
                for t in range(TT):
                    sp.dma_start(x_ln[:, t, :], x_f[n, :, t, :]).then_inc(x_in[t], 16)

            def residual(n, first=False, ahead=False, between={}):
                for t in range(TT):
                    if not first:
                        sp.wait_ge(mid_out[t], 16 * (n - 1))
                    sp.dma_start(x_res[:, t, :], x_f[n - 1, :, t, :]).then_inc(res_in[t], 16)
                if ahead:
                    load_x(n + 2)
                for i in between.get(-1, []):
                    fetch(i)
                for t in range(TT):
                    sp.wait_ge(m_free, m_base(n) + 5 + t)
                    sp.dma_start(mid_f[n - 1, :, t, :], x_res[:, t, :]).then_inc(mid_out[t], 16)
                    for i in between.get(t, []):
                        fetch(i)

            load_x(0, first=True)
            sp.dma_start(wq_stage[:, :, :], wq_t.rearrange("(k p) n -> p k n", p=P)).then_inc(wq_in, 16)
            sp.dma_start(ctx_stage[:, :, :], ctx_t.rearrange("(k p) n -> p k n", p=P)).then_inc(ctx_in, 16)
            sp.dma_start(wk_stage[:, :, :], wk_t.rearrange("(k p) n -> p k n", p=P)).then_inc(wk_in, 16)
            sp.dma_start(wv_stage[:, :, :], wv_t.rearrange("(k p) n -> p k n", p=P)).then_inc(wv_in, 16)
            ctx_p = ctx_t.rearrange("(k p) (b s) -> p k b s", p=P, b=B)
            for j in range(HG):
                for b in range(B):
                    sp.dma_start(ctx_rep[:, :, b, j * SK:(j + 1) * SK], ctx_p[:, :, b, :]).then_inc(rep_in, 16)
            sp.dma_start(wo_stage[:, :, :], wo_t.rearrange("(k p) n -> p k n", p=P)).then_inc(wo_in, 16)
            sp.wait_ge(t_full, 4)
            load_x(1, first=True)
            load_x(2)
            residual(1, first=True, ahead=True)
            with sp.Fori(2, NB - 2) as n:
                residual(n, ahead=True)
            residual(NB - 2)

            def fetch(i):
                if i >= 3:
                    sp.wait_ge(raw_used, i - 2)
                srcs, _ = PARTS[i]
                for src, cols in srcs:
                    if cols is None:
                        dst = raw[:, i % 3].rearrange("p k c -> p (k c)").rearrange("p (m d) -> p m d", d=D)
                    else:
                        dst = raw[:, i % 3, :, cols]
                    sp.dma_start(dst, src).then_inc(raw_in[i % 3], 16)

            def load_mid(n, slot):
                sp.dma_start(x2[:, slot], mid_f[n]).then_inc(x2_in[slot], 16)

            for i in range(3):
                fetch(i)
            residual(NB - 1, between={1: [3], 3: [4]})
            sp.wait_ge(s1_full, 4 * NB)
            load_mid(0, 0)
            load_mid(1, 1)
            residual(NB, between={-1: [5, 6], 1: [7], 3: [8]})
            for i in range(9, len(PARTS)):
                fetch(i)

            def store(n, slot):
                for t in range(TT):
                    sp.wait_ge(m_free, M_P2 + 4 * n + t + 1)
                    sp.dma_start(out_f[n, :, t, :], x2[:, slot, t, :]).then_inc(out_done[slot], 16)

            with sp.Fori(0, NB // 2 - 1) as i:
                for s in range(2):
                    store(2 * i + s, s)
                    sp.wait_ge(out_done[s], 64 * i + 64)
                    load_mid(2 * i + s + 2, s)
            for s in range(2):
                store(NB - 2 + s, s)
            for s in range(2):
                sp.wait_ge(out_done[s], 64 * (NB // 2))

        @block.gpsimd
        def _(pool):
            steps = [0]

            def step(ins):
                steps[0] += 1
                ins.then_inc(const_step, 1)
                pool.wait_ge(const_step, steps[0])

            def select(t, pattern, base, channel, fill, op):
                step(nc.gpsimd.affine_select(out=t, in_=t, compare_op=op, fill=fill, base=base,
                                             pattern=pattern, channel_multiplier=channel))

            nc.gpsimd.memset(half[:, :], -0.5).then_inc(half_ready, 1)
            step(nc.gpsimd.memset(ident[:, :], 0.0))
            select(ident[:, :], [[-1, P]], 0, 1, 1.0, ALU.not_equal)

            def normalise(n):
                pool.wait_ge(stats_ready, 4 * n + 4)
                pool.sem_inc(pool_passed, 1)
                nc.gpsimd.tensor_scalar(rstd[:, :], mv[:, :, 1], 1.0, EPS, ALU.mult, ALU.add).then_inc(var_eps, 1)
                nc.gpsimd.tensor_scalar(nmean[:, :], mv[:, :, 0], -1.0, 0.0, ALU.mult, ALU.add).then_inc(var_eps, 1)
                pool.wait_ge(var_eps, 2 * n + 2)
                nc.gpsimd.tensor_tensor(rstd[:, :], rstd[:, :], half[:, :], ALU.pow).then_inc(rstd_ready, 1)
                pool.wait_ge(rstd_ready, n + 1)
                pool.sem_inc(pool_passed, 1)
                for t in range(TT):
                    nc.gpsimd.tensor_scalar(x_ln[:, t, :], x_ln[:, t, :], nmean[:, t:t + 1], rstd[:, t:t + 1],
                                            ALU.add, ALU.mult).then_inc(x_normed, 1)

            def probabilities(n, t):
                for u, (rden_ready, p_ready) in enumerate(((rden0_ready, p0_ready), (rden1_ready, p1_ready))):
                    hs = slice(u * UH, (u + 1) * UH)
                    pool.wait_ge(rden_ready, 4 * n + t + 1)
                    nc.gpsimd.tensor_tensor(e[:, t % 2, hs], e[:, t % 2, hs],
                                            rden[:, t % 2, hs].unsqueeze(2).to_broadcast([P, UH, SK]),
                                            ALU.mult).then_inc(p_ready, 1)

            pool.wait_ge(half_ready, 1)
            normalise(0)

            step(nc.gpsimd.memset(k_mask[:, :, :], 1.0))
            select(k_mask[:, :, :], [[-HD, HG], [0, SK]], 0, 1, 0.0, ALU.is_ge)
            select(k_mask[:, :, :], [[HD, HG], [0, SK]], HD - 1, -1, 0.0, ALU.is_ge)
            step(nc.gpsimd.memset(v_mask[:, :, :, :], 1.0))
            for c in range(3):
                m = v_mask[:, c]
                select(m, [[-SK, HG], [0, HD]], CS[c], 1, 0.0, ALU.is_ge)
                select(m, [[SK, HG], [0, HD]], SK - 1 - CS[c], -1, 0.0, ALU.is_ge)
            select(v_mask[:, 2], [[0, HG], [0, HD]], -(2 * CH - CS[2]), 1, 0.0, ALU.is_ge)
            step(nc.gpsimd.memset(causal[:, :, :], 0.0))
            nc.gpsimd.affine_select(out=causal[:, :, :], in_=causal[:, :, :], compare_op=ALU.is_ge, fill=NEG, base=0,
                                    pattern=[[0, HG], [-1, SK]], channel_multiplier=1).then_inc(consts_ready, 1)

            normalise(1)
            for t in range(TT):
                probabilities(0, t)
            normalise(2)
            with pool.Fori(1, NB - 2) as n:
                for t in range(TT):
                    probabilities(n, t)
                normalise(n + 2)
            for t in range(TT):
                probabilities(NB - 2, t)

            def rstd2(n):
                pool.wait_ge(stats2_ready, 4 * n + 4)
                pool.sem_inc(pool_passed, 1)
                nc.gpsimd.tensor_scalar(rstd[:, :], mv[:, :, 1], 1.0, EPS, ALU.mult, ALU.add).then_inc(var2_eps, 1)
                pool.wait_ge(var2_eps, n + 1)
                nc.gpsimd.tensor_tensor(rstd[:, :], rstd[:, :], half[:, :], ALU.pow).then_inc(rstd2_ready, 1)

            got = [0, 0, 0]

            def convert(i):
                srcs, dst = PARTS[i]
                got[i % 3] += 16 * len(srcs)
                pool.wait_ge(raw_in[i % 3], got[i % 3])
                src = raw[:, i % 3]
                if len(srcs) == 1:
                    src = src.rearrange("p k c -> p (k c)").rearrange("p (m d) -> p m d", d=D)
                nc.gpsimd.tensor_copy(dst, src).then_inc(raw_used, 1)

            pool.wait_ge(m_full, m_base(NB - 1))
            for t in range(TT):
                probabilities(NB - 1, t)
                convert(t)
            rstd2(0)
            for i in range(TT, MH):
                convert(i)
            pool.wait_ge(m_full, M_LAST + 4)

            def h_low(n, m):
                pool.wait_ge(h_hi, MH * n + m + 1)
                nc.gpsimd.tensor_tensor(hT[:, 1, m, :], hid[:, m % 2, :], hT[:, 0, m, :].bitcast(f32),
                                        ALU.subtract).then_inc(h_lo, 1)

            left = list(range(MH, len(PARTS)))
            for m in range(MH):
                h_low(0, m)
                if left:
                    convert(left.pop(0))
                if m == 6:
                    rstd2(1)
            with pool.Fori(1, NB - 1) as n:
                for m in range(MH):
                    h_low(n, m)
                    if m == 6:
                        rstd2(n + 1)
            for m in range(MH):
                h_low(NB - 1, m)

        @block.scalar
        def _(act):
            act.dma_start(gates[:, 0:1], g_xattn).then_inc(gates_in, 16)
            act.dma_start(gates[:, 1:2], g_ffn).then_inc(gates_in, 16)
            act.wait_ge(gates_in, 32)
            nc.scalar.activation(gate_t[:, :], gates[:, :], ACT.Tanh).then_inc(gates_tanh, 1)

            def split_hi(n_arrived, arrived, dst, src):
                act.wait_ge(arrived, n_arrived)
                nc.scalar.activation(dst, src, ACT.Copy).then_inc(w_hi, 1)

            split_hi(16, wq_in, wq[:, 0], wq_stage[:, :, :])

            def kv_high(i, dst, src):
                act.wait_ge(kv_full, i + 1)
                nc.scalar.activation(dst, src, ACT.Copy).then_inc(kv_hi, 1)

            def t_high(i, slot, dst, src_rows=P):
                act.wait_ge(t_full, i + 1)
                src = t_bank[slot % 2][0:src_rows, :].rearrange("p (c n) -> p c n", c=4)
                nc.scalar.activation(dst, src, ACT.Copy).then_inc(t_hi, 1)

            def x_high(i, t, dst=None):
                t_high(i, t, (xT if dst is None else dst)[:, 0, :, t * P:(t + 1) * P])

            def p_high(n, t, r, at):
                t_high(t_base(n) + at, at, pT[0:CH, 0, 4 * r:4 * r + 4, t * P:(t + 1) * P], CH)

            def m_high(i, slot, dst):
                act.wait_ge(m_full, i + 1)
                nc.scalar.activation(dst, m_bank[slot % 2][:, :], ACT.Copy).then_inc(m_hi, 1)

            def exp0(n, t):
                act.wait_ge(s0_shifted, 4 * n + t + 1)
                nc.scalar.activation(e[:, t % 2, 0:UH, :], e[:, t % 2, 0:UH, :], ACT.Exp, scale=SCALE)\
                    .then_inc(exp0_done, 1)

            def exp1(n, t, between=None):
                act.wait_ge(nmx_ready, 4 * n + t + 1)
                for h in range(UH):
                    last = nc.scalar.activation(
                        e[:, t % 2, UH + h, :], s_bank[1][:, h // HG, (h % HG) * SK:(h % HG + 1) * SK], ACT.Exp,
                        bias=nmx[:, t % 2, h:h + 1], scale=SCALE, accum_out=den[:, t % 2, UH + h:UH + h + 1])
                    if h == UH // 2 - 1 and between is not None:
                        between()
                last.then_inc(exp1_done, 1)

            for t in range(TT):
                x_high(t, t)
            for m in range(G):
                for b in range(B):
                    i = B * m + b
                    kv_high(i, K[:, 0, b, m, :], k_full[:, i % 2].rearrange("p h k -> p (h k)"))
            for m in range(G):
                m_high(4 + m, m, qT[:, 0, m, :])
            split_hi(16, wo_in, wo[:, 0], wo_stage[:, :, :])

            def step(n, values, query):
                pt_at = 4 if query else 0

                def p(t, r):
                    p_high(n, t, r, pt_at + 3 * t + r)

                exp0(n, 0)
                if values == "first":
                    for c in range(3 * B):
                        kv_high(G * B + c, V[0:CH, 0, c // 3, :, :].rearrange("p (m c) n -> p m c n", c=3)[:, :, c % 3, :],
                                v_full[0:CH, c % 2])
                    exp1(n, 0)
                    for t in range(TT):
                        x_high(t_base(n) + t, t)
                else:
                    def weighted(m):
                        m_high(m_base(n) + m, m, aT[:, 0, m, :])
                        if query:
                            x_high(t_base(n) + m, m)
                    weighted(0)
                    exp1(n, 0, lambda: weighted(1))
                    weighted(2)
                    weighted(3)
                for t in (1, 2):
                    p(t - 1, 0)
                    exp0(n, t)
                    p(t - 1, 1)
                    exp1(n, t)
                    p(t - 1, 2)
                q_at = (m_base(n) + 8) if values != "first" else M_Q1

                def q(m):
                    if query:
                        m_high(q_at + m, m, qT[:, 0, m, :])

                p(2, 0)
                exp0(n, 3)
                p(2, 1)
                exp1(n, 3, lambda: q(0))
                p(2, 2)
                q(1)
                q(2)
                p(3, 0)
                q(3)
                p(3, 1)
                p(3, 2)

            step(0, "first", True)
            with act.Fori(1, NB - 1) as n:
                step(n, "loop", True)
            step(NB - 1, "loop", False)
            for m in range(G):
                m_high(M_LAST + m, m, aT[:, 0, m, :])
                if m >= 2:
                    x_high(T_P2 + m - 2, m - 2, xT2)

            for t in (2, 3):
                x_high(T_P2 + t, t, xT2)

            def tanh_gate(n, m):
                act.wait_ge(gu_full, MH * n + m + 1)
                nc.scalar.activation(th[:, m % 2, :], psum[:, 2 * (m % 2), :], ACT.Tanh, scale=0.5 * W_SCALE)\
                    .then_inc(tanh_done, 1)

            def h_high(n, m):
                act.wait_ge(gu_free, MH * n + m + 1)
                nc.scalar.activation(hT[:, 0, m, :], hid[:, m % 2, :], ACT.Copy).then_inc(h_hi, 1)

            def ffn(n, more):
                tanh_gate(n, 0)
                for m in range(MH):
                    if m + 1 < MH:
                        tanh_gate(n, m + 1)
                    h_high(n, m)
                if more:
                    for t in range(TT):
                        x_high(T_P2 + 4 * n + 4 + t, t, xT2)

            ffn(0, True)
            with act.Fori(1, NB - 1) as n:
                ffn(n, True)
            ffn(NB - 1, False)

        @block.vector
        def _(dve):
            def stats(n, t):
                dve.wait_ge(x_in[t], 16 * n + 16)
                nc.vector.bn_stats(bn[:, t, :], x_ln[:, t, :]).then_inc(bn_done, 1)
                dve.wait_ge(bn_done, 4 * n + t + 1)
                dve.sem_inc(dve_passed, 1)
                nc.vector.bn_aggr(mv[:, t, :], bn[:, t, :]).then_inc(stats_ready, 1)

            def split_lo(i, dst, src, hi):
                dve.wait_ge(w_hi, i)
                nc.vector.tensor_tensor(dst, src, hi.bitcast(f32), ALU.subtract).then_inc(w_split, 1)

            def t_low(i, slot, dst, hi, rows=P):
                dve.wait_ge(t_hi, i + 1)
                src = t_bank[slot % 2][0:rows, :].rearrange("p (c n) -> p c n", c=4)
                nc.vector.tensor_tensor(dst, src, hi.bitcast(f32), ALU.subtract).then_inc(t_free, 1)

            def x_low(i, t, of=None):
                of = xT if of is None else of
                c = slice(t * P, (t + 1) * P)
                t_low(i, t, of[:, 1, :, c], of[:, 0, :, c])

            def p_low(n, t, r, at):
                c = slice(t * P, (t + 1) * P)
                rr = slice(4 * r, 4 * r + 4)
                t_low(t_base(n) + at, at, pT[0:CH, 1, rr, c], pT[0:CH, 0, rr, c], CH)

            def m_low(hi_count, slot, dst, hi):
                dve.wait_ge(m_hi, hi_count)
                nc.vector.tensor_tensor(dst, m_bank[slot % 2][:, :], hi.bitcast(f32), ALU.subtract)\
                    .then_inc(m_free, 1)

            def v_low(n, m):
                m_low(h_base(n) + m + 1, m, aT[:, 1, m, :], aT[:, 0, m, :])

            def q_low(hi_count, m):
                m_low(hi_count, m, qT[:, 1, m, :], qT[:, 0, m, :])

            def unit(u):
                return s_bank[u][:, :, 0:GK].rearrange("p g (h k) -> p g h k", h=HG)

            def shift(n, t):
                dve.wait_ge(s0_full, 4 * n + t + 1)
                nc.vector.reduce_max(mx[:, t % 2, 0:UH], unit(0), AX.X).then_inc(mx0_done, 1)
                dve.wait_ge(mx0_done, 4 * n + t + 1)
                for g in range(2):
                    last = nc.vector.tensor_tensor(
                        e[:, t % 2, g * HG:(g + 1) * HG, :], unit(0)[:, g],
                        mx[:, t % 2, g * HG:(g + 1) * HG].unsqueeze(2).to_broadcast([P, HG, SK]), ALU.subtract)
                last.then_inc(s0_shifted, 1)
                dve.wait_ge(s1_full, 4 * n + t + 1)
                nc.vector.reduce_max(mx[:, t % 2, UH:H], unit(1), AX.X).then_inc(mx1_done, 1)
                dve.wait_ge(mx1_done, 4 * n + t + 1)
                nc.vector.tensor_scalar(nmx[:, t % 2, :], mx[:, t % 2, UH:H], -SCALE, None, ALU.mult)\
                    .then_inc(nmx_ready, 1)

            def slot_free(n, t, query):
                if t >= 2:
                    dve.wait_ge(t_full, t_base(n) + (4 if query else 0) + 3 * (t - 1))
                else:
                    dve.wait_ge(t_full, t_base(n) - 3 + 3 * t)

            def denominator0(n, t):
                dve.wait_ge(exp0_done, 4 * n + t + 1)
                nc.vector.reduce_sum(den[:, t % 2, 0:UH], e[:, t % 2, 0:UH, :], AX.X).then_inc(sum_done, 1)
                dve.wait_ge(sum_done, 4 * n + t + 1)
                nc.vector.reciprocal(rden[:, t % 2, 0:UH], den[:, t % 2, 0:UH]).then_inc(rden0_ready, 1)

            def denominator1(n, t):
                dve.wait_ge(exp1_done, 4 * n + t + 1)
                nc.vector.reciprocal(rden[:, t % 2, UH:H], den[:, t % 2, UH:H]).then_inc(rden1_ready, 1)

            def residual(n, t):
                dve.wait_ge(m_full, m_base(n) + 5 + t)
                dve.wait_ge(res_in[t], 16 * n)
                nc.vector.scalar_tensor_tensor(x_res[:, t, :], m_bank[t % 2][:, :], gate_t[:, 0:1], x_res[:, t, :],
                                               ALU.mult, ALU.add).then_inc(m_free, 1)

            for t in range(TT):
                stats(0, t)
            split_lo(1, wq[:, 1], wq_stage[:, :, :], wq[:, 0])
            for t in range(TT):
                x_low(t, t)
            dve.wait_ge(const_step, 5)
            for m in range(G):
                dve.wait_ge(m_full, m + 1)
                for b in range(B):
                    i = B * m + b
                    full = k_full[:, i % 2]
                    nc.vector.tensor_tensor(
                        full, m_bank[m % 2][:, b * SK:(b + 1) * SK].unsqueeze(1).to_broadcast([P, HG, SK]),
                        k_mask[:, :, :], ALU.mult).then_inc(kv_full, 1)
                    dve.wait_ge(kv_full, i + 1)
                    dve.wait_ge(kv_hi, i + 1)
                    low = nc.vector.tensor_tensor(K[:, 1, b, m, :], full.rearrange("p h k -> p (h k)"),
                                                  K[:, 0, b, m, :].bitcast(f32), ALU.subtract)
                low.then_inc(m_free, 1)
            for m in range(G):
                q_low(m + 1, m)
            split_lo(2, wo[:, 1], wo_stage[:, :, :], wo[:, 0])
            dve.wait_ge(gates_tanh, 1)
            nc.vector.tensor_scalar(gate_ffn[:, :], gate_t[:, 1:2], 0.5 * W_SCALE ** 3, None, ALU.mult)\
                .then_inc(gate_ready, 1)

            def step(n, values, query, ahead):
                first = values == "first"
                pt_at = 4 if query else 0

                def p(t, r):
                    p_low(n, t, r, pt_at + 3 * t + r)

                def res(t):
                    if not first:
                        residual(n, t)

                def st(t):
                    if ahead:
                        stats(n + 2, t)

                if not first:
                    slot_free(n, 0, query)
                shift(n, 0)
                if first:
                    dve.wait_ge(consts_ready, 1)
                    for c in range(3 * B):
                        full = v_full[0:CH, c % 2]
                        i = G * B + c
                        dve.wait_ge(m_full, V_AT + c + 1)
                        nc.vector.tensor_tensor(
                            full, m_bank[c % 2][0:CH, :].rearrange("p (m n) -> p m n", m=G),
                            v_mask[0:CH, c % 3].rearrange("p h d -> p (h d)").unsqueeze(1).to_broadcast([CH, G, P]),
                            ALU.mult).then_inc(kv_full, 1)
                        dve.wait_ge(kv_full, i + 1)
                        dve.wait_ge(kv_hi, i + 1)
                        lo, hi = (V[0:CH, q, c // 3].rearrange("p (m c) n -> p m c n", c=3)[:, :, c % 3, :]
                                  for q in (1, 0))
                        nc.vector.tensor_tensor(lo, full, hi.bitcast(f32), ALU.subtract).then_inc(m_free, 1)
                    denominator0(n, 0)
                    denominator1(n, 0)
                    for t in range(TT):
                        x_low(t_base(n) + t, t)
                else:
                    for m in range(G):
                        v_low(n, m)
                        if query:
                            x_low(t_base(n) + m, m)
                        if m == 0:
                            denominator0(n, 0)
                        if m == 1:
                            denominator1(n, 0)
                    slot_free(n, 1, query)
                shift(n, 1)
                p(0, 0)
                denominator0(n, 1)
                p(0, 1)
                res(0)
                denominator1(n, 1)
                p(0, 2)
                st(0)
                res(1)
                slot_free(n, 2, query)
                shift(n, 2)
                p(1, 0)
                denominator0(n, 2)
                p(1, 1)
                res(2)
                denominator1(n, 2)
                p(1, 2)
                st(1)
                res(3)
                slot_free(n, 3, query)
                shift(n, 3)
                q_at = (h_base(n) + 5) if not first else 5

                def q(m):
                    if query:
                        q_low(q_at + m, m)

                p(2, 0)
                denominator0(n, 3)
                p(2, 1)
                st(2)
                q(0)
                denominator1(n, 3)
                p(2, 2)
                st(3)
                q(1)
                q(2)
                p(3, 0)
                q(3)
                p(3, 1)
                p(3, 2)

            for t in range(TT):
                stats(1, t)
            step(0, "first", True, True)
            with dve.Fori(1, NB - 2) as n:
                step(n, "loop", True, True)
            step(NB - 2, "loop", True, False)
            step(NB - 1, "loop", False, False)
            def stats2(n, slot, t, arrived):
                if t == 0:
                    dve.wait_ge(x2_in[slot], arrived)
                nc.vector.bn_stats(bn[:, t, :], x2[:, slot, t, :]).then_inc(bn2_done, 1)
                dve.wait_ge(bn2_done, 4 * n + t + 1)
                dve.sem_inc(dve_passed, 1)
                nc.vector.bn_aggr(mv[:, t, :], bn[:, t, :]).then_inc(stats2_ready, 1)

            def normalise2(n, slot):
                dve.wait_ge(rstd2_ready, n + 1)
                for t in range(TT):
                    nc.vector.tensor_scalar(xh[:, t, :], x2[:, slot, t, :], mv[:, t, 0:1], rstd[:, t:t + 1],
                                            ALU.subtract, ALU.mult).then_inc(x2_normed, 1)

            def hidden(n, m):
                dve.wait_ge(tanh_done, MH * n + m + 1)
                nc.vector.scalar_tensor_tensor(th[:, m % 2, :], th[:, m % 2, :], 1.0, psum[:, 2 * (m % 2), :],
                                               ALU.add, ALU.mult).then_inc(silu_done, 1)
                dve.wait_ge(silu_done, MH * n + m + 1)
                if m < 2:
                    if not (isinstance(n, int) and n == 0):
                        dve.wait_ge(h_lo, MH * n + m - 1)
                else:
                    dve.wait_ge(h_lo, MH * n + m - 1)
                nc.vector.tensor_tensor(hid[:, m % 2, :], th[:, m % 2, :], psum[:, 2 * (m % 2) + 1, :], ALU.mult)\
                    .then_inc(gu_free, 1)

            def result(n, slot, t):
                dve.wait_ge(m_full, M_P2 + 4 * n + t + 1)
                nc.vector.scalar_tensor_tensor(x2[:, slot, t, :], m_bank[t % 2][:, :], gate_ffn[:, 0:1],
                                               x2[:, slot, t, :], ALU.mult, ALU.add).then_inc(m_free, 1)

            def ffn(n, slot, arrived, more):
                for m in range(MH):
                    hidden(n, m)
                    if more and 2 <= m < 2 + TT:
                        stats2(n + 1, 1 - slot, m - 2, arrived)
                    if more and m == 8:
                        normalise2(n + 1, 1 - slot)
                for t in (0, 1):
                    if more:
                        x_low(T_P2 + 4 * n + 4 + t, t, xT2)
                result(n, slot, 0)
                for t in (2, 3):
                    if more:
                        x_low(T_P2 + 4 * n + 4 + t, t, xT2)
                for t in range(1, TT):
                    result(n, slot, t)

            for t in range(TT):
                stats2(0, 0, t, 16)
            for m in range(G):
                m_low(H_LAST + m + 1, m, aT[:, 1, m, :], aT[:, 0, m, :])
                if m == 0:
                    normalise2(0, 0)
                if m >= 2:
                    x_low(T_P2 + m - 2, m - 2, xT2)
            residual(NB, 0)
            x_low(T_P2 + 2, 2, xT2)
            residual(NB, 1)
            x_low(T_P2 + 3, 3, xT2)
            residual(NB, 2)
            residual(NB, 3)
            dve.wait_ge(gate_ready, 1)
            ffn(0, 0, 16, True)
            with dve.Fori(0, NB // 2 - 1) as i:
                ffn(2 * i + 1, 1, 16 * i + 32, True)
                ffn(2 * i + 2, 0, 16 * i + 32, True)
            ffn(NB - 1, 1, 0, False)

        @block.tensor
        def _(pe):
            def product(dst, terms):
                for j, (stat, mov) in enumerate(terms):
                    last = nc.tensor.matmul(dst, stat, mov, start=(j == 0), stop=(j == len(terms) - 1))
                return last

            CROSS = ((0, 0), (1, 0), (0, 1))

            def t_wait(i, always=False):
                if always or not (isinstance(i, int) and i < 2):
                    pe.wait_ge(t_free, i - 1)

            def m_wait(i):
                if not (isinstance(i, int) and i < 2):
                    pe.wait_ge(m_free, i - 1)

            def transpose_x(i, t, normed, ready, src):
                pe.wait_ge(ready, normed)
                t_wait(i)
                for k in range(KD):
                    last = nc.tensor.transpose(t_bank[t % 2][:, k * P:(k + 1) * P], src[:, t, k * P:(k + 1) * P],
                                               ident[:, :])
                last.then_inc(t_full, 1)

            def transpose_p(n, t, r, at):
                if r < 2:
                    pe.wait_ge((p0_ready, p1_ready)[r], 4 * n + t + 1)
                t_wait(t_base(n) + at)
                rows = e[:, t % 2].rearrange("p h k -> p (h k)")
                for j in range(4):
                    g, c = divmod(4 * r + j, 3)
                    last = nc.tensor.transpose(t_bank[at % 2][0:CH, j * P:(j + 1) * P],
                                               rows[:, g * GK + CS[c]:g * GK + CS[c] + CH], ident[:, :])
                last.then_inc(t_full, 1)

            def query(i, m):
                m_wait(i)
                product(m_bank[m % 2][:, :],
                        [(wq[:, a, k, m * P:(m + 1) * P], xT[:, c, k, :]) for k in range(KD) for a, c in CROSS]
                        ).then_inc(m_full, 1)

            def scores(n, t, b, masked, rows=None):
                for u in range(2):
                    if rows is not None:
                        pe.wait_ge(m_free, rows[u])
                    if not (isinstance(n, int) and n == 0 and t == 0):
                        pe.wait_ge((s0_shifted, exp1_done)[u], 4 * n + t)
                    for g in range(2):
                        m = 2 * u + g
                        terms = [(qT[:, a, m, t * P:(t + 1) * P], K[:, c, b, m, :]) for a, c in CROSS]
                        if masked:
                            terms.append((ident[:, :], causal[:, :, :].rearrange("p h k -> p (h k)")))
                        last = product(s_bank[u][:, g, 0:GK], terms)
                    last.then_inc((s0_full, s1_full)[u], 1)

            def values(i, m, b, split):
                pe.wait_ge(t_free, split)
                m_wait(i)
                product(m_bank[m % 2][:, :],
                        [(V[0:CH, a, b, 3 * m + c, :], pT[0:CH, d, 3 * m + c, :]) for c in range(3) for a, d in CROSS]
                        ).then_inc(m_full, 1)

            def project(i, t):
                m_wait(i)
                product(m_bank[t % 2][:, :],
                        [(aT[:, a, m, t * P:(t + 1) * P], wo[:, c, m, :]) for m in range(G) for a, c in CROSS]
                        ).then_inc(m_full, 1)

            pe.wait_ge(const_step, 2)
            for t in range(TT):
                transpose_x(t, t, t + 1, x_normed, x_ln)
            pe.wait_ge(ctx_in, 16)
            pe.wait_ge(wk_in, 16)
            for m in range(G):
                m_wait(m)
                product(m_bank[m % 2][:, 0:B * SK],
                        [(wk_stage[:, k, m * P:(m + 1) * P], ctx_stage[:, k, :]) for k in range(KD)]
                        ).then_inc(m_full, 1)
            pe.wait_ge(w_split, 1)
            pe.wait_ge(t_free, 4)
            for m in range(G):
                query(4 + m, m)
            pe.wait_ge(consts_ready, 1)

            def step(n, b, b_before, masked, first, more):
                base = None if first else m_base(n)
                q_at = M_Q1 if first else base + 8
                pt_at = 4 if more else 0

                def p(t, r):
                    transpose_p(n, t, r, pt_at + 3 * t + r)

                def xt(t):
                    if more:
                        transpose_x(t_base(n) + t, t, 4 * n + 5 + t, x_normed, x_ln)

                def o(t):
                    if not first:
                        project(base + 4 + t, t)

                def q(m):
                    if more:
                        query(q_at + m, m)

                scores(n, 0, b, masked, (8, 8) if first else (m_base(n) - 2, m_base(n)))
                if first:
                    pe.wait_ge(wv_in, 16)
                    pe.wait_ge(rep_in, 16 * HG * B)
                    for c in range(3 * B):
                        m_wait(V_AT + c)
                        product(m_bank[c % 2][0:CH, :],
                                [(ctx_rep[:, k, c // 3, CS[c % 3]:CS[c % 3] + CH], wv_stage[:, k, :])
                                 for k in range(KD)]).then_inc(m_full, 1)
                    pe.wait_ge(w_split, 2)
                    for t in range(TT):
                        xt(t)
                else:
                    for m in range(G):
                        values(base + m, m, b_before, t_base(n) - 2 + min(m, 2))
                        xt(m)
                scores(n, 1, b, False)
                p(0, 0)
                p(0, 1)
                if not first:
                    pe.wait_ge(m_free, base + 4)
                o(0)
                p(0, 2)
                o(1)
                scores(n, 2, b, False)
                p(1, 0)
                p(1, 1)
                o(2)
                p(1, 2)
                o(3)
                scores(n, 3, b, False)
                p(2, 0)
                p(2, 1)
                if more:
                    pe.wait_ge(t_free, t_base(n) + 4)
                q(0)
                p(2, 2)
                q(1)
                q(2)
                p(3, 0)
                q(3)
                p(3, 1)
                p(3, 2)

            step(0, 0, 0, True, True, True)
            for b in range(B):
                if b:
                    step(b * BPB, b, b - 1, True, False, True)
                with pe.Fori(b * BPB + 1, (b + 1) * BPB - (b == B - 1)) as n:
                    step(n, b, b, False, False, True)
            step(NB - 1, B - 1, B - 1, False, False, False)
            for m in range(G):
                values(M_LAST + m, m, B - 1, T_P2 - 2 + min(m, 2))
            for t in (0, 1):
                transpose_x(T_P2 + t, t, t + 1, x2_normed, xh)
            pe.wait_ge(m_free, M_LAST + 4)
            for t in range(TT):
                project(M_LAST + 4 + t, t)
                if t < 2:
                    transpose_x(T_P2 + 2 + t, 2 + t, 3 + t, x2_normed, xh)

            def gate_up(n, m, weights=None):
                if m < 2:
                    if not (isinstance(n, int) and n == 0):
                        pe.wait_ge(gu_free, MH * n + m - 1)
                else:
                    pe.wait_ge(gu_free, MH * n + m - 1)
                if weights is not None:
                    pe.wait_ge(raw_used, weights)
                for j in range(2):
                    c = (2 * m + j) * P
                    last = product(psum[:, 2 * (m % 2) + j, :],
                                   [(w_gu[:, k, c:c + P], xT2[:, a, k, :]) for k in range(KD) for a in range(2)])
                last.then_inc(gu_full, 1)

            def down(n, t):
                m_wait(M_P2 + 4 * n + t)
                terms = [(hT[:, a, m, t * P:(t + 1) * P], w_d[:, m, :]) for m in range(MH) for a in range(2)]
                for j, (stat, mov) in enumerate(terms):
                    if t == 0 and j % 2 == 0:
                        pe.wait_ge(h_lo, MH * n + j // 2 + 1)
                    last = nc.tensor.matmul(m_bank[t % 2][:, :], stat, mov, start=(j == 0), stop=(j == len(terms) - 1))
                last.then_inc(m_full, 1)

            def ffn(n, more, first=False):
                pe.wait_ge(t_free, T_P2 + 4 * n + 4)
                for m in range(MH):
                    gate_up(n, m, m + 1 if first else None)
                def xt(t):
                    if more:
                        transpose_x(T_P2 + 4 * n + 4 + t, t, 4 * n + 5 + t, x2_normed, xh)

                xt(0)
                xt(1)
                if first:
                    pe.wait_ge(raw_used, len(PARTS))
                down(n, 0)
                xt(2)
                xt(3)
                for t in range(1, TT):
                    down(n, t)

            ffn(0, True, True)
            with pe.Fori(1, NB - 1) as n:
                ffn(n, True)
            ffn(NB - 1, False)


def kernel(**inputs):
    import numpy as np
    import concourse.bacc as bacc
    from concourse.bass_utils import run_bass_kernel_spmd as run

    def t(name):
        return np.ascontiguousarray(np.asarray(inputs[name]).T)

    c = np.asarray(inputs["ctx_1024"])
    x = np.ascontiguousarray(inputs["x"])
    arrays = {
        "x": x,
        "ctx_t": np.ascontiguousarray(c.reshape(-1, c.shape[2]).T),
        "g_xattn": np.ascontiguousarray(np.broadcast_to(np.asarray(inputs["g_xattn"]).reshape(1, 1), (128, 1))),
        "g_ffn": np.ascontiguousarray(np.broadcast_to(np.asarray(inputs["g_ffn"]).reshape(1, 1), (128, 1))),
        "wq_t": t("L0_xattn_Wq"), "wk_t": t("L0_xattn_Wk"), "wv_t": t("L0_xattn_Wv"), "wo_t": t("L0_xattn_Wo"),
        "w_gate_t": t("L0_ffn_w_gate"), "w_up_t": t("L0_ffn_w_up"), "w_down_t": t("L0_ffn_w_down"),
    }
    nc = bacc.Bacc("TRN2", target_bir_lowering=False, num_devices=1,
                   dynamic_dma_scratch_size=1024)
    args = [nc.dram_tensor(n, a.shape, mybir.dt.from_np(a.dtype), kind="ExternalInput").ap() for n, a in arrays.items()]
    args.append(nc.dram_tensor("x_mid", (x.shape[0] * x.shape[1], x.shape[2]), mybir.dt.float32, kind="Internal").ap())
    args.append(nc.dram_tensor("out", x.shape, mybir.dt.float32, kind="ExternalOutput").ap())
    flamingo_gated_block(nc, *args)
    r = run(nc, [arrays], core_ids=[0])
    return r.results[0]["out"]
```

```python
import concourse.bass as bass
from concourse import mybir
from contextlib import ExitStack


def flamingo_gated_block(
    nc: bass.Bass,
    x: bass.AP,
    ctx_t: bass.AP,
    g_xattn: bass.AP,
    g_ffn: bass.AP,
    wq_t: bass.AP,
    wk_t: bass.AP,
    wv_t: bass.AP,
    wo_t: bass.AP,
    w_gate_t: bass.AP,
    w_up_t: bass.AP,
    w_down_t: bass.AP,
    x_mid: bass.AP,
    out: bass.AP,
):
    f32, f32r, i32 = mybir.dt.float32, mybir.dt.float32r, mybir.dt.int32
    ALU = mybir.AluOpType
    ACT = mybir.ActivationFunctionType
    AX = mybir.AxisListType

    P = 128
    B, SQ, D = x.shape
    SK = ctx_t.shape[1] // B
    HID = w_gate_t.shape[1]
    H, HD = 16, 32
    SCALE = HD ** -0.5
    NEG = -1e9
    EPS = 1e-5
    W_SCALE = 1.0 / 127.0
    KD = D // P
    TT = 4
    TB = TT * P
    NB = B * SQ // TB
    BPB = SQ // TB
    HG = P // HD
    G = H // HG
    GK = HG * SK
    UH = H // 2
    CH = -(-GK // 3)
    CS = [0, CH, GK - CH]
    NC = 3 * G
    MH = HID // P
    EXACT = 2.0 ** 12
    NT = B * SQ // P

    x_f = x.rearrange("b s d -> (b s) d").rearrange("(n t p) d -> n p t d", p=P, t=TT)
    out_f = out.rearrange("b s d -> (b s) d").rearrange("(n t p) d -> n p t d", p=P, t=TT)
    out_t = out.rearrange("b s d -> (b s) d").rearrange("(n p) d -> n p d", p=P)
    mid_t = x_mid.rearrange("(n p) d -> n p d", p=P)
    mid_f = x_mid.rearrange("(n t p) d -> n p t d", p=P, t=TT)

    def t_base(n):
        return 4 + 16 * n

    V_AT = 4
    M_Q1 = V_AT + B

    def m_base(n):
        return M_Q1 + 4 + 12 * (n - 1) - (4 if isinstance(n, int) and n == NB else 0)

    def h_base(n):
        return 8 + 8 * (n - 1)

    T_P2 = t_base(NB - 1) + 12
    M_LAST = m_base(NB)
    M_P2 = M_LAST + 8
    H_LAST = h_base(NB - 1) + 4

    ctx = ExitStack()
    with ctx:
        def sb(name, shape, dt=f32, where=ctx):
            return where.enter_context(nc.sbuf_tensor(name, shape, dt))

        def sem(name):
            return ctx.enter_context(nc.semaphore(name))

        ident = sb("ident", [P, P])
        causal = sb("causal", [P, HG, SK])
        gates = sb("gates", [P, 2])
        gate_t = sb("gate_t", [P, 2])
        gate_ffn = sb("gate_ffn", [P, 1])
        bn = sb("bn", [P, TT, 6])
        mv = sb("mv", [P, TT, 2])
        rstd = sb("rstd", [P, TT])
        nmean = sb("nmean", [P, TT])
        half = sb("half", [P, TT])
        mx = sb("mx", [P, 2, H])
        nmx = sb("nmx", [P, 2, UH])
        den = sb("den", [P, 2, H])
        rden = sb("rden", [P, 2, H])
        w_parts = MH + MH // 2
        w_max = sb("w_max", [P, w_parts])
        w_top = sb("w_top", [P, 1])
        wide_f = sb("wide_f", [1, 1])
        wide = sb("wide", [1, 1], i32)
        raw = sb("raw", [P, 3, KD, P * 2], i32)

        with ExitStack() as a1:
            wq = sb("wq", [P, 2, KD, D], f32r, a1)
            xT = sb("xT", [P, 2, KD, TB], f32r, a1)
            x_ln = sb("x_ln", [P, TT, D], f32, a1)
            wv_stage = sb("wv_stage", [P, KD, D], f32, a1)
        with ExitStack() as a2:
            wide_gu = sb("wide_gu", [P, KD, 2, HID], f32, a2)
        w_gu = sb("w_gu", [P, KD, 2 * HID], f32r)
        with ExitStack() as b1:
            qT = sb("qT", [P, 2, G, TB], f32r, b1)
            K = sb("K", [P, 2, B, G, GK], f32r, b1)
            e = sb("e", [P, 2, H, SK], f32, b1)
        with ExitStack() as b2:
            x2 = sb("x2", [P, 2, TT, D], f32, b2)
            xh = sb("xh", [P, TT, D], f32, b2)
            xT2 = sb("xT2", [P, 2, KD, TB], f32r, b2)
        with ExitStack() as b3:
            wide_x = sb("wide_x", [P, D], f32, b3)
            wide_xh = sb("wide_xh", [P, D], f32, b3)
            wide_xT = sb("wide_xT", [P, KD, P], f32, b3)
            wide_th = sb("wide_th", [P, 2, P], f32, b3)
            wide_h = sb("wide_h", [P, MH, P], f32, b3)
        sb("region_b", [P, 2 * G * TB + 2 * B * G * GK + 2 * H * SK])
        with ExitStack() as c0:
            wq_stage = sb("wq_stage", [P, KD, D], f32, c0)
            wk_stage = sb("wk_stage", [P, KD, D], f32, c0)
            ctx_stage = sb("ctx_stage", [P, KD, B * SK], f32, c0)
        with ExitStack() as c1:
            pT = sb("pT", [P, 2, NC, TB], f32r, c1)
        with ExitStack() as c2:
            wide_raw = sb("wide_raw", [P, KD * 2 * HID], i32, c2)
        hT = sb("hT", [P, 2, MH, TB], f32r)
        with ExitStack() as d1:
            V = sb("V", [P, 2, B, NC, P], f32r, d1)
        with ExitStack() as d2:
            wide_d = sb("wide_d", [P, MH, D], f32, d2)
        w_d = sb("w_d", [P, MH, D], f32r)
        with ExitStack() as e0:
            v_keys = sb("v_keys", [P, B, D], f32, e0)
            v_full = sb("v_full", [P, B, NC, P], f32, e0)
        with ExitStack() as e2:
            th = sb("th", [P, 2, TB], f32, e2)
            hid = sb("hid", [P, 2, TB], f32, e2)
        aT = sb("aT", [P, 2, G, TB], f32r)
        wo = sb("wo", [P, 2, KD, D], f32r)
        x_res = sb("x_res", [P, TT, D])

        psum = ctx.enter_context(nc.psum_tensor("psum", [P, 8, 512], f32))
        s_bank = [psum[:, 0:2, :], psum[:, 2:4, :]]
        t_bank = [psum[:, 4, :], psum[:, 5, :]]
        m_bank = [psum[:, 6, :], psum[:, 7, :]]

        consts_ready = sem("consts_ready")
        const_step = sem("const_step")
        half_ready = sem("half_ready")
        gates_in = sem("gates_in")
        gates_tanh = sem("gates_tanh")
        gate_ready = sem("gate_ready")
        wk_in, wv_in, wo_in = sem("wk_in"), sem("wv_in"), sem("wo_in")
        wq_in = [sem(f"wq_in{k}") for k in range(KD)]
        ctx_in = sem("ctx_in")
        w_hi = sem("w_hi")
        w_split, wo_split = sem("w_split"), sem("wo_split")
        k_zero, v_zero = sem("k_zero"), sem("v_zero")
        k_full, k_hi, k_split = sem("k_full"), sem("k_hi"), sem("k_split")
        v_in = [sem(f"v_in{b}") for b in range(B)]
        v_hi, v_split = sem("v_hi"), sem("v_split")
        x_in = [sem(f"x_in{t}") for t in range(TT)]
        bn_done = sem("bn_done")
        stats_ready = sem("stats_ready")
        var_eps = sem("var_eps")
        rstd_ready = sem("rstd_ready")
        x_normed = sem("x_normed")
        dve_passed, pool_passed, sp_passed = sem("dve_passed"), sem("pool_passed"), sem("sp_passed")
        t_full, t_hi, t_free = sem("t_full"), sem("t_hi"), sem("t_free")
        m_full, m_hi, m_free = sem("m_full"), sem("m_hi"), sem("m_free")
        s0_full, s1_full = sem("s0_full"), sem("s1_full")
        mx0_done, mx1_done = sem("mx0_done"), sem("mx1_done")
        s0_shifted = sem("s0_shifted")
        nmx_ready = sem("nmx_ready")
        exp0_done, exp1_done = sem("exp0_done"), sem("exp1_done")
        sum_done = sem("sum_done")
        rden0_ready, rden1_ready = sem("rden0_ready"), sem("rden1_ready")
        p0_ready, p1_ready = sem("p0_ready"), sem("p1_ready")
        res_in = [sem(f"res_in{t}") for t in range(TT)]
        mid_out = [sem(f"mid_out{t}") for t in range(TT)]
        raw_in = [sem(f"raw_in{i}") for i in range(3)]
        raw_used = [sem(f"raw_used{i}") for i in range(3)]
        x2_in = [sem(f"x2_in{i}") for i in range(2)]
        bn2_done, stats2_ready = sem("bn2_done"), sem("stats2_ready")
        var2_eps, rstd2_ready = sem("var2_eps"), sem("rstd2_ready")
        x2_normed = sem("x2_normed")
        gu_full, tanh_done, gu_free = sem("gu_full"), sem("tanh_done"), sem("gu_free")
        silu_done = sem("silu_done")
        h_hi, h_lo = sem("h_hi"), sem("h_lo")
        w_max_done, w_top_done = sem("w_max_done"), sem("w_top_done")
        w_top_row = sem("w_top_row")
        top_done, wide_cmp = sem("top_done"), sem("wide_cmp")
        wide_ready = sem("wide_ready")
        wide_raw_in, wide_converted = sem("wide_raw_in"), sem("wide_converted")
        wide_x_in, wide_out = sem("wide_x_in"), sem("wide_out")
        wide_bn, wide_stats, wide_eps, wide_rstd = (sem(n) for n in ("wide_bn", "wide_stats", "wide_eps", "wide_rstd"))
        wide_normed, wide_t, wide_xt_ready = sem("wide_normed"), sem("wide_t"), sem("wide_xt_ready")
        wide_gu_full, wide_tanh, wide_silu = sem("wide_gu_full"), sem("wide_tanh"), sem("wide_silu")
        wide_hid, wide_down, wide_result = sem("wide_hid"), sem("wide_down"), sem("wide_result")
        out_done = [sem(f"out_done{i}") for i in range(2)]

        def raw_parts():
            gate = w_gate_t.rearrange("(k p) h -> p k h", p=P)
            up = w_up_t.rearrange("(k p) h -> p k h", p=P)
            down = w_down_t.rearrange("(k p) d -> p k d", p=P)
            parts = []
            for m in range(MH):
                c = slice(m * P, (m + 1) * P)
                parts.append(([(gate[:, :, c], slice(0, P)), (up[:, :, c], slice(P, 2 * P))],
                              w_gu[:, :, 2 * P * m:2 * P * (m + 1)]))
            for m in range(0, MH, 2):
                parts.append(([(down[:, m:m + 2, :], None)], w_d[:, m:m + 2, :]))
            return parts

        PARTS = raw_parts()

        def v_places():
            places = []
            for c in range(3):
                start = CS[c] if c == 0 else CS[c - 1] + CH
                for j in range(HG):
                    lo, hi = max(j * SK, start), min((j + 1) * SK, CS[c] + CH)
                    if lo < hi:
                        places.append((c, j, lo - CS[c], lo - j * SK, hi - lo))
            return places

        V_PLACES = v_places()

        def too_wide(eng):
            eng.wait_ge(wide_ready, 1)
            return eng.value_load(wide[0:1, 0:1], min_val=0, max_val=1) == 1

        def raw_copy(i):
            srcs, dst = PARTS[i]
            src = raw[:, i % 3]
            if len(srcs) == 1:
                src = src.rearrange("p k c -> p (k c)").rearrange("p (m d) -> p m d", d=D)
            return dst, src

        def raw_arrived(i):
            return 16 * sum(len(PARTS[j][0]) for j in range(i % 3, i + 1, 3))

        block = ctx.enter_context(nc.Block())

        @block.sync
        def _(sp):
            def load_x(n, first=False):
                if not first:
                    sp.wait_ge(t_full, t_base(n - 2) + 4)
                for t in range(TT):
                    sp.dma_start(x_ln[:, t, :], x_f[n, :, t, :]).then_inc(x_in[t], 16)

            def load_mid(n, slot):
                sp.dma_start(x2[:, slot], mid_f[n]).then_inc(x2_in[slot], 16)

            def residual(n, first=False, ahead=False, between={}, mid_after=None):
                for t in range(TT):
                    if not first:
                        sp.wait_ge(mid_out[t], 16 * (n - 1))
                    sp.dma_start(x_res[:, t, :], x_f[n - 1, :, t, :]).then_inc(res_in[t], 16)
                if ahead:
                    load_x(n + 2)
                for i in between.get(-1, []):
                    fetch(i)
                for t in range(TT):
                    sp.wait_ge(m_free, m_base(n) + 5 + t)
                    sp.dma_start(mid_f[n - 1, :, t, :], x_res[:, t, :]).then_inc(mid_out[t], 16)
                    for i in between.get(t, []):
                        fetch(i)
                    if mid_after == t:
                        sp.wait_ge(s1_full, 4 * NB)
                        load_mid(0, 0)

            load_x(0, first=True)
            sp.dma_start(ctx_stage[:, :, :], ctx_t.rearrange("(k p) n -> p k n", p=P)).then_inc(ctx_in, 16)
            sp.dma_start(wk_stage[:, :, :], wk_t.rearrange("(k p) n -> p k n", p=P)).then_inc(wk_in, 16)
            for k in range(KD):
                sp.dma_start(wq_stage[:, k, :], wq_t[k * P:(k + 1) * P, :]).then_inc(wq_in[k], 16)
            sp.dma_start(wv_stage[:, :, :], wv_t.rearrange("(k p) n -> p k n", p=P)).then_inc(wv_in, 16)
            sp.wait_ge(t_full, 4)
            load_x(1, first=True)
            sp.dma_start(x_res[:, :, :], wo_t.rearrange("(k p) n -> p k n", p=P)).then_inc(wo_in, 16)
            sp.wait_ge(v_zero, 1)
            for b in range(B):
                sp.wait_ge(m_free, V_AT + b + 1)
                to = v_full[:, b].rearrange("p (m c) n -> p m c n", c=3)
                of = v_keys[:, b].rearrange("p (m n) -> p m n", m=G)
                for c, j, row, key, rows in V_PLACES:
                    sp.dma_start(to[row:row + rows, :, c, j * HD:(j + 1) * HD],
                                 of[key:key + rows, :, j * HD:(j + 1) * HD]).then_inc(v_in[b], 16)
                if b == 0:
                    load_x(2)
            sp.wait_ge(wo_split, 2)
            residual(1, first=True, ahead=True)
            with sp.Fori(2, NB - 2) as n:
                residual(n, ahead=True)
            residual(NB - 2)

            def fetch(i):
                if i >= 3:
                    sp.wait_ge(raw_used[i % 3], i // 3)
                srcs, _ = PARTS[i]
                for src, cols in srcs:
                    if cols is None:
                        dst = raw[:, i % 3].rearrange("p k c -> p (k c)").rearrange("p (m d) -> p m d", d=D)
                    else:
                        dst = raw[:, i % 3, :, cols]
                    sp.dma_start(dst, src).then_inc(raw_in[i % 3], 16)

            for i in range(3):
                fetch(i)
            residual(NB - 1, between={-1: [3], 0: [4], 1: [5], 2: [6], 3: [7, 8]}, mid_after=1)
            residual(NB, between={-1: [9, 10, 11, 12], 1: [13], 3: [14]})
            load_mid(1, 1)
            for i in range(15, len(PARTS)):
                fetch(i)
            for t in range(TT):
                sp.wait_ge(mid_out[t], 16 * NB)

            def store(n, slot):
                for t in range(TT):
                    sp.wait_ge(m_free, M_P2 + 4 * n + t + 1)
                    sp.dma_start(out_f[n, :, t, :], x2[:, slot, t, :]).then_inc(out_done[slot], 16)

            with sp.Fori(0, NB // 2 - 1) as i:
                for s in range(2):
                    store(2 * i + s, s)
                    sp.wait_ge(out_done[s], 64 * i + 64)
                    load_mid(2 * i + s + 2, s)
            for s in range(2):
                store(NB - 2 + s, s)
            for s in range(2):
                sp.wait_ge(out_done[s], 64 * (NB // 2))

            with sp.If(too_wide(sp)):
                gu_raw = wide_raw[:, :].rearrange("p (k j h) -> p k j h", k=KD, j=2)
                for j, w in enumerate((w_gate_t, w_up_t)):
                    sp.dma_start(gu_raw[:, :, j, :], w.rearrange("(k p) h -> p k h", p=P)).then_inc(wide_raw_in, 16)
                sp.wait_ge(wide_converted, 1)
                sp.dma_start(wide_raw[:, 0:MH * D].rearrange("p (m d) -> p m d", d=D),
                             w_down_t.rearrange("(m p) d -> p m d", p=P)).then_inc(wide_raw_in, 16)
                with sp.Fori(0, NT) as n:
                    sp.dma_start(wide_x[:, :], mid_t[n]).then_inc(wide_x_in, 16)
                    sp.wait_ge(wide_result, n + 1)
                    sp.sem_inc(sp_passed, 1)
                    sp.dma_start(out_t[n], wide_x[:, :]).then_inc(wide_out, 16)
                    sp.wait_ge(wide_out, 16 * n + 16)
                    sp.sem_inc(sp_passed, 1)

        @block.gpsimd
        def _(pool):
            steps = [0]

            def step(ins):
                steps[0] += 1
                ins.then_inc(const_step, 1)
                pool.wait_ge(const_step, steps[0])

            def select(t, pattern, base, channel, fill, op):
                step(nc.gpsimd.affine_select(out=t, in_=t, compare_op=op, fill=fill, base=base,
                                             pattern=pattern, channel_multiplier=channel))

            nc.gpsimd.memset(half[:, :], -0.5).then_inc(half_ready, 1)
            step(nc.gpsimd.memset(ident[:, :], 0.0))
            select(ident[:, :], [[-1, P]], 0, 1, 1.0, ALU.not_equal)
            nc.gpsimd.memset(K[:, :, :, :, :].bitcast(f32), 0.0).then_inc(k_zero, 1)

            def normalise(n):
                pool.wait_ge(stats_ready, 4 * n + 4)
                pool.sem_inc(pool_passed, 1)
                nc.gpsimd.tensor_scalar(rstd[:, :], mv[:, :, 1], 1.0, EPS, ALU.mult, ALU.add).then_inc(var_eps, 1)
                nc.gpsimd.tensor_scalar(nmean[:, :], mv[:, :, 0], -1.0, 0.0, ALU.mult, ALU.add).then_inc(var_eps, 1)
                pool.wait_ge(var_eps, 2 * n + 2)
                nc.gpsimd.tensor_tensor(rstd[:, :], rstd[:, :], half[:, :], ALU.pow).then_inc(rstd_ready, 1)
                pool.wait_ge(rstd_ready, n + 1)
                pool.sem_inc(pool_passed, 1)
                for t in range(TT):
                    nc.gpsimd.tensor_scalar(x_ln[:, t, :], x_ln[:, t, :], nmean[:, t:t + 1], rstd[:, t:t + 1],
                                            ALU.add, ALU.mult).then_inc(x_normed, 1)

            def probabilities(n, t):
                for u, (rden_ready, p_ready) in enumerate(((rden0_ready, p0_ready), (rden1_ready, p1_ready))):
                    hs = slice(u * UH, (u + 1) * UH)
                    pool.wait_ge(rden_ready, 4 * n + t + 1)
                    nc.gpsimd.tensor_tensor(e[:, t % 2, hs], e[:, t % 2, hs],
                                            rden[:, t % 2, hs].unsqueeze(2).to_broadcast([P, UH, SK]),
                                            ALU.mult).then_inc(p_ready, 1)

            pool.wait_ge(half_ready, 1)
            normalise(0)

            step(nc.gpsimd.memset(causal[:, :, :], 0.0))
            nc.gpsimd.affine_select(out=causal[:, :, :], in_=causal[:, :, :], compare_op=ALU.is_ge, fill=NEG, base=0,
                                    pattern=[[0, HG], [-1, SK]], channel_multiplier=1).then_inc(consts_ready, 1)
            nc.gpsimd.memset(v_full[0:CH], 0.0).then_inc(v_zero, 1)

            for j in range(2):
                pool.wait_ge(w_hi, KD + j + 1)
                ks = slice(2 * j, 2 * j + 2)
                nc.gpsimd.tensor_tensor(wo[:, 1, ks], x_res[:, ks, :], wo[:, 0, ks].bitcast(f32),
                                        ALU.subtract).then_inc(wo_split, 1)
            normalise(1)
            for t in range(TT):
                probabilities(0, t)
            for b in range(1, B):
                pool.wait_ge(v_hi, b + 1)
                nc.gpsimd.tensor_tensor(V[0:CH, 1, b], v_full[0:CH, b], V[0:CH, 0, b].bitcast(f32),
                                        ALU.subtract).then_inc(v_split, 1)
            normalise(2)
            with pool.Fori(1, NB - 2) as n:
                for t in range(TT):
                    probabilities(n, t)
                normalise(n + 2)
            for t in range(TT):
                probabilities(NB - 2, t)

            def rstd2(n):
                pool.wait_ge(stats2_ready, 4 * n + 4)
                pool.sem_inc(pool_passed, 1)
                nc.gpsimd.tensor_scalar(rstd[:, :], mv[:, :, 1], 1.0, EPS, ALU.mult, ALU.add).then_inc(var2_eps, 1)
                pool.wait_ge(var2_eps, n + 1)
                nc.gpsimd.tensor_tensor(rstd[:, :], rstd[:, :], half[:, :], ALU.pow).then_inc(rstd2_ready, 1)

            def convert(i):
                pool.wait_ge(raw_in[i % 3], raw_arrived(i))
                nc.gpsimd.tensor_copy(*raw_copy(i)).then_inc(raw_used[i % 3], 1)

            pool.wait_ge(m_full, m_base(NB - 1))
            for t in range(TT):
                probabilities(NB - 1, t)
                if t < 2:
                    convert(2 * t)
            convert(6)
            rstd2(0)
            for i in (8, 10):
                convert(i)
            pool.wait_ge(m_full, M_LAST + 4)

            def h_low(n, m):
                pool.wait_ge(h_hi, MH * n + m + 1)
                nc.gpsimd.tensor_tensor(hT[:, 1, m, :], hid[:, m % 2, :], hT[:, 0, m, :].bitcast(f32),
                                        ALU.subtract).then_inc(h_lo, 1)

            for m in range(MH):
                h_low(0, m)
                if m == 6:
                    rstd2(1)
            with pool.Fori(1, NB - 1) as n:
                for m in range(MH):
                    h_low(n, m)
                    if m == 6:
                        rstd2(n + 1)
            for m in range(MH):
                h_low(NB - 1, m)

            with pool.If(too_wide(pool)):
                with pool.Fori(0, NT) as n:
                    pool.wait_ge(wide_stats, n + 1)
                    pool.sem_inc(pool_passed, 1)
                    nc.gpsimd.tensor_scalar(rstd[:, 0:1], mv[:, 0, 1:2], 1.0, EPS, ALU.mult, ALU.add)\
                        .then_inc(wide_eps, 1)
                    pool.wait_ge(wide_eps, n + 1)
                    nc.gpsimd.tensor_tensor(rstd[:, 0:1], rstd[:, 0:1], half[:, 0:1], ALU.pow).then_inc(wide_rstd, 1)

        @block.scalar
        def _(act):
            act.dma_start(gates[:, 0:1], g_xattn).then_inc(gates_in, 16)
            act.dma_start(gates[:, 1:2], g_ffn).then_inc(gates_in, 16)
            act.wait_ge(gates_in, 32)
            nc.scalar.activation(gate_t[:, :], gates[:, :], ACT.Tanh).then_inc(gates_tanh, 1)

            def split_hi(arrived, dst, src):
                act.wait_ge(arrived, 16)
                nc.scalar.activation(dst, src, ACT.Copy).then_inc(w_hi, 1)

            def k_high(m):
                act.wait_ge(k_full, m + 1)
                for j in range(HG):
                    rows = slice(j * HD, (j + 1) * HD)
                    last = nc.scalar.activation(K[rows, 0, :, m, j * SK:(j + 1) * SK],
                                                psum[rows, m, 0:B * SK].rearrange("p (b s) -> p b s", b=B),
                                                ACT.Copy)
                last.then_inc(k_hi, 1)

            def v_high(b):
                act.wait_ge(v_in[b], 16 * len(V_PLACES))
                nc.scalar.activation(V[0:CH, 0, b], v_full[0:CH, b], ACT.Copy).then_inc(v_hi, 1)

            def wo_high(j):
                split_hi(wo_in, wo[:, 0, 2 * j:2 * j + 2], x_res[:, 2 * j:2 * j + 2, :])

            def t_high(i, slot, dst, src_rows=P):
                act.wait_ge(t_full, i + 1)
                src = t_bank[slot % 2][0:src_rows, :].rearrange("p (c n) -> p c n", c=4)
                nc.scalar.activation(dst, src, ACT.Copy).then_inc(t_hi, 1)

            def x_high(i, t, dst=None):
                t_high(i, t, (xT if dst is None else dst)[:, 0, :, t * P:(t + 1) * P])

            def p_high(n, t, r, at):
                t_high(t_base(n) + at, at, pT[0:CH, 0, 4 * r:4 * r + 4, t * P:(t + 1) * P], CH)

            def m_high(i, slot, dst):
                act.wait_ge(m_full, i + 1)
                nc.scalar.activation(dst, m_bank[slot % 2][:, :], ACT.Copy).then_inc(m_hi, 1)

            def exp0(n, t):
                act.wait_ge(s0_shifted, 4 * n + t + 1)
                nc.scalar.activation(e[:, t % 2, 0:UH, :], e[:, t % 2, 0:UH, :], ACT.Exp, scale=SCALE)\
                    .then_inc(exp0_done, 1)

            def exp1(n, t, between=None):
                act.wait_ge(nmx_ready, 4 * n + t + 1)
                for h in range(UH):
                    last = nc.scalar.activation(
                        e[:, t % 2, UH + h, :], s_bank[1][:, h // HG, (h % HG) * SK:(h % HG + 1) * SK], ACT.Exp,
                        bias=nmx[:, t % 2, h:h + 1], scale=SCALE, accum_out=den[:, t % 2, UH + h:UH + h + 1])
                    if h == UH // 2 - 1 and between is not None:
                        between()
                last.then_inc(exp1_done, 1)

            x_high(0, 0)
            x_high(1, 1)
            split_hi(wq_in[0], wq[:, 0, 0], wq_stage[:, 0, :])
            split_hi(wq_in[1], wq[:, 0, 1], wq_stage[:, 1, :])
            x_high(2, 2)
            x_high(3, 3)
            split_hi(wq_in[2], wq[:, 0, 2], wq_stage[:, 2, :])
            split_hi(wq_in[3], wq[:, 0, 3], wq_stage[:, 3, :])
            act.wait_ge(k_zero, 1)
            for m in range(G):
                if m < 2:
                    k_high(2 * m)
                    k_high(2 * m + 1)
                else:
                    wo_high(m - 2)
                m_high(m, m, qT[:, 0, m, :])

            def convert(i):
                act.wait_ge(raw_in[i % 3], raw_arrived(i))
                nc.scalar.activation(*raw_copy(i), ACT.Copy).then_inc(raw_used[i % 3], 1)

            def step(n, first, query):
                pt_at = 4 if query else 0

                def p(t, r):
                    p_high(n, t, r, pt_at + 3 * t + r)
                    if r == 2 and not query:
                        if t == 0:
                            act.wait_ge(m_full, m_base(NB - 1))
                        convert((1, 3, 4, 5)[t])

                exp0(n, 0)
                if first:
                    exp1(n, 0)
                    for t in range(TT):
                        x_high(t_base(n) + t, t)
                else:
                    def weighted(m):
                        m_high(m_base(n) + m, m, aT[:, 0, m, :])
                        if query:
                            x_high(t_base(n) + m, m)
                    weighted(0)
                    exp1(n, 0, lambda: weighted(1))
                    weighted(2)
                    weighted(3)
                q_at = M_Q1 if first else m_base(n) + 8

                def q(m):
                    if query:
                        m_high(q_at + m, m, qT[:, 0, m, :])

                for t in (1, 2):
                    p(t - 1, 0)
                    exp0(n, t)
                    p(t - 1, 1)
                    exp1(n, t)
                    p(t - 1, 2)
                if first:
                    v_high(0)
                    exp0(n, 3)
                    q(0)
                    p(2, 0)
                    v_high(1)
                    p(2, 1)
                    exp1(n, 3)
                    q(1)
                    p(2, 2)
                    q(2)
                    p(3, 0)
                    p(3, 1)
                    q(3)
                    p(3, 2)
                else:
                    p(2, 0)
                    exp0(n, 3)
                    p(2, 1)
                    exp1(n, 3, lambda: q(0))
                    p(2, 2)
                    q(1)
                    q(2)
                    p(3, 0)
                    q(3)
                    p(3, 1)
                    p(3, 2)

            step(0, True, True)
            with act.Fori(1, NB - 1) as n:
                step(n, False, True)
            step(NB - 1, False, False)
            for m in range(G):
                m_high(M_LAST + m, m, aT[:, 0, m, :])
                if m == 1:
                    convert(7)
            x_high(T_P2, 0, xT2)
            x_high(T_P2 + 1, 1, xT2)
            convert(9)
            x_high(T_P2 + 2, 2, xT2)
            convert(11)
            x_high(T_P2 + 3, 3, xT2)
            act.wait_ge(m_full, M_LAST + 4)

            def tanh_gate(n, m):
                act.wait_ge(gu_full, MH * n + m + 1)
                nc.scalar.activation(th[:, m % 2, :], psum[:, 2 * (m % 2), :], ACT.Tanh, scale=0.5 * W_SCALE)\
                    .then_inc(tanh_done, 1)

            def h_high(n, m):
                act.wait_ge(gu_free, MH * n + m + 1)
                nc.scalar.activation(hT[:, 0, m, :], hid[:, m % 2, :], ACT.Copy).then_inc(h_hi, 1)

            def ffn(n, more, first=False):
                tanh_gate(n, 0)
                for m in range(MH):
                    if m + 1 < MH:
                        tanh_gate(n, m + 1)
                    h_high(n, m)
                    if first and MH + m < len(PARTS):
                        convert(MH + m)
                if more:
                    for t in range(TT):
                        x_high(T_P2 + 4 * n + 4 + t, t, xT2)

            ffn(0, True, True)
            with act.Fori(1, NB - 1) as n:
                ffn(n, True)
            ffn(NB - 1, False)

            with act.If(too_wide(act)):
                with act.Fori(0, NT) as n:
                    for m in range(MH):
                        act.wait_ge(wide_gu_full, MH * n + m + 1)
                        nc.scalar.activation(wide_th[:, m % 2, :], psum[:, 2 * (m % 2), 0:P], ACT.Tanh,
                                             scale=0.5 * W_SCALE).then_inc(wide_tanh, 1)

        @block.vector
        def _(dve):
            def stats(n, t):
                dve.wait_ge(x_in[t], 16 * n + 16)
                nc.vector.bn_stats(bn[:, t, :], x_ln[:, t, :]).then_inc(bn_done, 1)
                dve.wait_ge(bn_done, 4 * n + t + 1)
                dve.sem_inc(dve_passed, 1)
                nc.vector.bn_aggr(mv[:, t, :], bn[:, t, :]).then_inc(stats_ready, 1)

            def split_lo(i, dst, src, hi):
                dve.wait_ge(w_hi, i)
                nc.vector.tensor_tensor(dst, src, hi.bitcast(f32), ALU.subtract).then_inc(w_split, 1)

            def t_low(i, slot, dst, hi, rows=P):
                dve.wait_ge(t_hi, i + 1)
                src = t_bank[slot % 2][0:rows, :].rearrange("p (c n) -> p c n", c=4)
                nc.vector.tensor_tensor(dst, src, hi.bitcast(f32), ALU.subtract).then_inc(t_free, 1)

            def x_low(i, t, of=None):
                of = xT if of is None else of
                c = slice(t * P, (t + 1) * P)
                t_low(i, t, of[:, 1, :, c], of[:, 0, :, c])

            def p_low(n, t, r, at):
                c = slice(t * P, (t + 1) * P)
                rr = slice(4 * r, 4 * r + 4)
                t_low(t_base(n) + at, at, pT[0:CH, 1, rr, c], pT[0:CH, 0, rr, c], CH)

            def m_low(hi_count, slot, dst, hi):
                dve.wait_ge(m_hi, hi_count)
                nc.vector.tensor_tensor(dst, m_bank[slot % 2][:, :], hi.bitcast(f32), ALU.subtract)\
                    .then_inc(m_free, 1)

            def v_low(n, m):
                m_low(h_base(n) + m + 1, m, aT[:, 1, m, :], aT[:, 0, m, :])

            def q_low(hi_count, m):
                m_low(hi_count, m, qT[:, 1, m, :], qT[:, 0, m, :])

            def unit(u):
                return s_bank[u][:, :, 0:GK].rearrange("p g (h k) -> p g h k", h=HG)

            def shift(n, t):
                dve.wait_ge(s0_full, 4 * n + t + 1)
                nc.vector.reduce_max(mx[:, t % 2, 0:UH], unit(0), AX.X).then_inc(mx0_done, 1)
                dve.wait_ge(mx0_done, 4 * n + t + 1)
                for g in range(2):
                    last = nc.vector.tensor_tensor(
                        e[:, t % 2, g * HG:(g + 1) * HG, :], unit(0)[:, g],
                        mx[:, t % 2, g * HG:(g + 1) * HG].unsqueeze(2).to_broadcast([P, HG, SK]), ALU.subtract)
                last.then_inc(s0_shifted, 1)
                dve.wait_ge(s1_full, 4 * n + t + 1)
                nc.vector.reduce_max(mx[:, t % 2, UH:H], unit(1), AX.X).then_inc(mx1_done, 1)
                dve.wait_ge(mx1_done, 4 * n + t + 1)
                nc.vector.tensor_scalar(nmx[:, t % 2, :], mx[:, t % 2, UH:H], -SCALE, None, ALU.mult)\
                    .then_inc(nmx_ready, 1)

            def slot_free(n, t, query):
                if t >= 2:
                    dve.wait_ge(t_full, t_base(n) + (4 if query else 0) + 3 * (t - 1))
                else:
                    dve.wait_ge(t_full, t_base(n) - 3 + 3 * t)

            def denominator0(n, t):
                dve.wait_ge(exp0_done, 4 * n + t + 1)
                nc.vector.reduce_sum(den[:, t % 2, 0:UH], e[:, t % 2, 0:UH, :], AX.X).then_inc(sum_done, 1)
                dve.wait_ge(sum_done, 4 * n + t + 1)
                nc.vector.reciprocal(rden[:, t % 2, 0:UH], den[:, t % 2, 0:UH]).then_inc(rden0_ready, 1)

            def denominator1(n, t):
                dve.wait_ge(exp1_done, 4 * n + t + 1)
                nc.vector.reciprocal(rden[:, t % 2, UH:H], den[:, t % 2, UH:H]).then_inc(rden1_ready, 1)

            def residual(n, t):
                dve.wait_ge(m_full, m_base(n) + 5 + t)
                dve.wait_ge(res_in[t], 16 * n)
                nc.vector.scalar_tensor_tensor(x_res[:, t, :], m_bank[t % 2][:, :], gate_t[:, 0:1], x_res[:, t, :],
                                               ALU.mult, ALU.add).then_inc(m_free, 1)

            for t in range(TT):
                stats(0, t)

            def k_low(m):
                dve.wait_ge(k_hi, m + 1)
                for j in range(HG):
                    rows = slice(j * HD, (j + 1) * HD)
                    c = slice(j * SK, (j + 1) * SK)
                    last = nc.vector.tensor_tensor(K[rows, 1, :, m, c],
                                                   psum[rows, m, 0:B * SK].rearrange("p (b s) -> p b s", b=B),
                                                   K[rows, 0, :, m, c].bitcast(f32), ALU.subtract)
                last.then_inc(k_split, 1)

            def v_low_rows(b):
                dve.wait_ge(v_hi, b + 1)
                nc.vector.tensor_tensor(V[0:CH, 1, b], v_full[0:CH, b], V[0:CH, 0, b].bitcast(f32), ALU.subtract)\
                    .then_inc(v_split, 1)

            def wq_low(k):
                split_lo(k + 1, wq[:, 1, k], wq_stage[:, k, :], wq[:, 0, k])

            x_low(0, 0)
            x_low(1, 1)
            wq_low(0)
            wq_low(1)
            x_low(2, 2)
            x_low(3, 3)
            wq_low(2)
            wq_low(3)
            for m in range(G):
                if m < 2:
                    k_low(2 * m)
                    k_low(2 * m + 1)
                q_low(m + 1, m)
                stats(1, m)
            dve.wait_ge(gates_tanh, 1)
            nc.vector.tensor_scalar(gate_ffn[:, :], gate_t[:, 1:2], 0.5 * W_SCALE ** 3, None, ALU.mult)\
                .then_inc(gate_ready, 1)

            def stats2(n, slot, t, arrived):
                if t == 0:
                    dve.wait_ge(x2_in[slot], arrived)
                nc.vector.bn_stats(bn[:, t, :], x2[:, slot, t, :]).then_inc(bn2_done, 1)
                dve.wait_ge(bn2_done, 4 * n + t + 1)
                dve.sem_inc(dve_passed, 1)
                nc.vector.bn_aggr(mv[:, t, :], bn[:, t, :]).then_inc(stats2_ready, 1)

            def step(n, first, query, ahead):
                pt_at = 4 if query else 0

                def p(t, r):
                    p_low(n, t, r, pt_at + 3 * t + r)

                def res(t):
                    if not first:
                        residual(n, t)

                def st(t):
                    if ahead:
                        stats(n + 2, t)

                if not first:
                    slot_free(n, 0, query)
                shift(n, 0)
                if first:
                    def v_copy(b):
                        dve.wait_ge(m_full, V_AT + b + 1)
                        nc.vector.tensor_copy(v_keys[0:SK, b], m_bank[b % 2][0:SK, :]).then_inc(m_free, 1)

                    denominator0(n, 0)
                    v_copy(0)
                    denominator1(n, 0)
                    for t in range(TT):
                        x_low(t_base(n) + t, t)
                else:
                    for m in range(G):
                        v_low(n, m)
                        if query:
                            x_low(t_base(n) + m, m)
                        if m == 0:
                            denominator0(n, 0)
                        if m == 1:
                            denominator1(n, 0)
                    slot_free(n, 1, query)
                q_at = 5 if first else h_base(n) + 5

                def q(m):
                    if query:
                        q_low(q_at + m, m)

                shift(n, 1)
                p(0, 0)
                denominator0(n, 1)
                p(0, 1)
                res(0)
                denominator1(n, 1)
                if first:
                    v_copy(1)
                p(0, 2)
                if not first:
                    st(0)
                if query:
                    res(1)
                slot_free(n, 2, query)
                shift(n, 2)
                p(1, 0)
                denominator0(n, 2)
                p(1, 1)
                res(2 if query else 1)
                denominator1(n, 2)
                p(1, 2)
                if not first:
                    st(1)
                if query:
                    res(3)
                slot_free(n, 3, query)
                shift(n, 3)
                if first:
                    denominator0(n, 3)
                    q(0)
                    p(2, 0)
                    p(2, 1)
                    v_low_rows(0)
                    denominator1(n, 3)
                    q(1)
                    p(2, 2)
                    st(0)
                    st(1)
                    q(2)
                    st(2)
                    p(3, 0)
                    p(3, 1)
                    q(3)
                    st(3)
                    p(3, 2)
                else:
                    p(2, 0)
                    denominator0(n, 3)
                    p(2, 1)
                    st(2)
                    q(0)
                    if not query:
                        res(2)
                    denominator1(n, 3)
                    p(2, 2)
                    if not query:
                        res(3)
                    st(3)
                    q(1)
                    q(2)
                    p(3, 0)
                    q(3)
                    p(3, 1)
                    p(3, 2)
                    if not query:
                        stats2(0, 0, 0, 16)

            step(0, True, True, True)
            with dve.Fori(1, NB - 2) as n:
                step(n, False, True, True)
            step(NB - 2, False, True, False)
            step(NB - 1, False, False, False)
            def normalise2(n, slot, tiles=range(TT)):
                dve.wait_ge(rstd2_ready, n + 1)
                for t in tiles:
                    nc.vector.tensor_scalar(xh[:, t, :], x2[:, slot, t, :], mv[:, t, 0:1], rstd[:, t:t + 1],
                                            ALU.subtract, ALU.mult).then_inc(x2_normed, 1)

            def hidden(n, m):
                dve.wait_ge(tanh_done, MH * n + m + 1)
                nc.vector.scalar_tensor_tensor(th[:, m % 2, :], th[:, m % 2, :], 1.0, psum[:, 2 * (m % 2), :],
                                               ALU.add, ALU.mult).then_inc(silu_done, 1)
                dve.wait_ge(silu_done, MH * n + m + 1)
                if m < 2:
                    if not (isinstance(n, int) and n == 0):
                        dve.wait_ge(h_lo, MH * n + m - 1)
                else:
                    dve.wait_ge(h_lo, MH * n + m - 1)
                nc.vector.tensor_tensor(hid[:, m % 2, :], th[:, m % 2, :], psum[:, 2 * (m % 2) + 1, :], ALU.mult)\
                    .then_inc(gu_free, 1)

            def result(n, slot, t):
                dve.wait_ge(m_full, M_P2 + 4 * n + t + 1)
                nc.vector.scalar_tensor_tensor(x2[:, slot, t, :], m_bank[t % 2][:, :], gate_ffn[:, 0:1],
                                               x2[:, slot, t, :], ALU.mult, ALU.add).then_inc(m_free, 1)

            def largest(i, weights):
                nc.vector.reduce_max(w_max[:, i:i + 1], weights.bitcast(f32), AX.XY, apply_absolute_value=True)\
                    .then_inc(w_max_done, 1)

            def ffn(n, slot, arrived, more, first=False):
                for m in range(MH):
                    hidden(n, m)
                    if first:
                        largest(m, w_gu[:, :, 2 * P * m:2 * P * (m + 1)])
                    if not more and m < MH // 2:
                        largest(MH + m, w_d[:, 2 * m:2 * m + 2, :])
                    if not more and m == MH // 2:
                        dve.wait_ge(w_max_done, w_parts)
                        nc.vector.reduce_max(w_top[:, :], w_max[:, :], AX.X).then_inc(w_top_done, 1)
                    if not more and m == MH - 2:
                        dve.wait_ge(w_top_row, 1)
                        nc.vector.reduce_max(wide_f[:, :], t_bank[0][0:1, 0:P], AX.X).then_inc(top_done, 1)
                        dve.wait_ge(top_done, 1)
                        nc.vector.tensor_scalar(wide_f[:, :], wide_f[:, :], EXACT, None, ALU.is_ge)\
                            .then_inc(wide_cmp, 1)
                        dve.wait_ge(wide_cmp, 1)
                        nc.vector.tensor_copy(wide[:, :], wide_f[:, :]).then_inc(wide_ready, 1)
                    if more and 2 <= m < 2 + TT:
                        stats2(n + 1, 1 - slot, m - 2, arrived)
                    if more and m == 8:
                        normalise2(n + 1, 1 - slot)
                for t in (0, 1):
                    if more:
                        x_low(T_P2 + 4 * n + 4 + t, t, xT2)
                result(n, slot, 0)
                for t in (2, 3):
                    if more:
                        x_low(T_P2 + 4 * n + 4 + t, t, xT2)
                for t in range(1, TT):
                    result(n, slot, t)

            for m in range(G):
                m_low(H_LAST + m + 1, m, aT[:, 1, m, :], aT[:, 0, m, :])
                if m == 0:
                    stats2(0, 0, 1, 16)
                if m == 1:
                    stats2(0, 0, 2, 16)
                    stats2(0, 0, 3, 16)
                if m >= 2:
                    normalise2(0, 0, range(2 * (m - 2), 2 * (m - 2) + 2))
            x_low(T_P2, 0, xT2)
            x_low(T_P2 + 1, 1, xT2)
            residual(NB, 0)
            x_low(T_P2 + 2, 2, xT2)
            residual(NB, 1)
            x_low(T_P2 + 3, 3, xT2)
            residual(NB, 2)
            residual(NB, 3)
            dve.wait_ge(gate_ready, 1)
            ffn(0, 0, 16, True, True)
            with dve.Fori(0, NB // 2 - 1) as i:
                ffn(2 * i + 1, 1, 16 * i + 32, True)
                ffn(2 * i + 2, 0, 16 * i + 32, True)
            ffn(NB - 1, 1, 0, False)

            with dve.If(too_wide(dve)):
                dve.wait_ge(wide_raw_in, 32)
                nc.vector.tensor_copy(wide_gu[:, :, :, :].rearrange("p k j h -> p (k j h)"), wide_raw[:, :])\
                    .then_inc(wide_converted, 1)
                dve.wait_ge(wide_raw_in, 48)
                nc.vector.tensor_copy(wide_d[:, :, :].rearrange("p m d -> p (m d)"), wide_raw[:, 0:MH * D])\
                    .then_inc(wide_converted, 1)
                with dve.Fori(0, NT) as n:
                    dve.wait_ge(wide_x_in, 16 * n + 16)
                    nc.vector.bn_stats(bn[:, 0, :], wide_x[:, :]).then_inc(wide_bn, 1)
                    dve.wait_ge(wide_bn, n + 1)
                    dve.sem_inc(dve_passed, 1)
                    nc.vector.bn_aggr(mv[:, 0, :], bn[:, 0, :]).then_inc(wide_stats, 1)
                    dve.wait_ge(wide_rstd, n + 1)
                    nc.vector.tensor_scalar(wide_xh[:, :], wide_x[:, :], mv[:, 0, 0:1], rstd[:, 0:1],
                                            ALU.subtract, ALU.mult).then_inc(wide_normed, 1)
                    dve.wait_ge(wide_t, n + 1)
                    nc.vector.tensor_copy(wide_xT[:, :, :].rearrange("p k n -> p (k n)"), t_bank[0][:, :])\
                        .then_inc(wide_xt_ready, 1)
                    for m in range(MH):
                        dve.wait_ge(wide_tanh, MH * n + m + 1)
                        nc.vector.scalar_tensor_tensor(wide_th[:, m % 2, :], wide_th[:, m % 2, :], 1.0,
                                                       psum[:, 2 * (m % 2), 0:P], ALU.add, ALU.mult)\
                            .then_inc(wide_silu, 1)
                        dve.wait_ge(wide_silu, MH * n + m + 1)
                        nc.vector.tensor_tensor(wide_h[:, m, :], wide_th[:, m % 2, :],
                                                psum[:, 2 * (m % 2) + 1, 0:P], ALU.mult).then_inc(wide_hid, 1)
                    dve.wait_ge(wide_down, n + 1)
                    nc.vector.scalar_tensor_tensor(wide_x[:, :], m_bank[0][:, :], gate_ffn[:, 0:1], wide_x[:, :],
                                                   ALU.mult, ALU.add).then_inc(wide_result, 1)

        @block.tensor
        def _(pe):
            def product(dst, terms):
                for j, (stat, mov) in enumerate(terms):
                    last = nc.tensor.matmul(dst, stat, mov, start=(j == 0), stop=(j == len(terms) - 1))
                return last

            CROSS = ((0, 0), (1, 0), (0, 1))

            def t_wait(i, always=False):
                if always or not (isinstance(i, int) and i < 2):
                    pe.wait_ge(t_free, i - 1)

            def m_wait(i):
                if not (isinstance(i, int) and i < 2):
                    pe.wait_ge(m_free, i - 1)

            def transpose_x(i, t, normed, ready, src):
                pe.wait_ge(ready, normed)
                t_wait(i)
                for k in range(KD):
                    last = nc.tensor.transpose(t_bank[t % 2][:, k * P:(k + 1) * P], src[:, t, k * P:(k + 1) * P],
                                               ident[:, :])
                last.then_inc(t_full, 1)

            def transpose_p(n, t, r, at):
                if r < 2:
                    pe.wait_ge((p0_ready, p1_ready)[r], 4 * n + t + 1)
                t_wait(t_base(n) + at)
                rows = e[:, t % 2].rearrange("p h k -> p (h k)")
                for j in range(4):
                    g, c = divmod(4 * r + j, 3)
                    last = nc.tensor.transpose(t_bank[at % 2][0:CH, j * P:(j + 1) * P],
                                               rows[:, g * GK + CS[c]:g * GK + CS[c] + CH], ident[:, :])
                last.then_inc(t_full, 1)

            def query(i, m):
                m_wait(i)
                product(m_bank[m % 2][:, :],
                        [(wq[:, a, k, m * P:(m + 1) * P], xT[:, c, k, :]) for k in range(KD) for a, c in CROSS]
                        ).then_inc(m_full, 1)

            def scores(n, t, b, masked, rows=None):
                for u in range(2):
                    if rows is not None:
                        pe.wait_ge(m_free, rows[u])
                    if isinstance(n, int) and n == 0 and t == 0:
                        pe.wait_ge(k_split, 2 * u + 2)
                    if not (isinstance(n, int) and n == 0 and t == 0):
                        pe.wait_ge((s0_shifted, exp1_done)[u], 4 * n + t)
                    for g in range(2):
                        m = 2 * u + g
                        terms = [(qT[:, a, m, t * P:(t + 1) * P], K[:, c, b, m, :]) for a, c in CROSS]
                        if masked:
                            terms.append((ident[:, :], causal[:, :, :].rearrange("p h k -> p (h k)")))
                        last = product(s_bank[u][:, g, 0:GK], terms)
                    last.then_inc((s0_full, s1_full)[u], 1)

            def values(i, m, b, split):
                pe.wait_ge(t_free, split)
                m_wait(i)
                product(m_bank[m % 2][:, :],
                        [(V[0:CH, a, b, 3 * m + c, :], pT[0:CH, d, 3 * m + c, :]) for c in range(3) for a, d in CROSS]
                        ).then_inc(m_full, 1)

            def project(i, t):
                m_wait(i)
                product(m_bank[t % 2][:, :],
                        [(aT[:, a, m, t * P:(t + 1) * P], wo[:, c, m, :]) for m in range(G) for a, c in CROSS]
                        ).then_inc(m_full, 1)

            pe.wait_ge(const_step, 2)


            def keys(m):
                product(psum[:, m, 0:B * SK],
                        [(wk_stage[:, k, m * P:(m + 1) * P], ctx_stage[:, k, :]) for k in range(KD)]
                        ).then_inc(k_full, 1)

            for t in (0, 1):
                transpose_x(t, t, t + 1, x_normed, x_ln)
            pe.wait_ge(ctx_in, 16)
            pe.wait_ge(wk_in, 16)
            keys(0)
            for t in (2, 3):
                transpose_x(t, t, t + 1, x_normed, x_ln)
            for m in range(1, G):
                keys(m)
            pe.wait_ge(w_split, KD)
            pe.wait_ge(t_free, 4)
            for m in range(G):
                query(m, m)
            pe.wait_ge(consts_ready, 1)

            def step(n, b, b_before, masked, first, more):
                base = None if first else m_base(n)
                q_at = M_Q1 if first else base + 8
                pt_at = 4 if more else 0

                def p(t, r):
                    transpose_p(n, t, r, pt_at + 3 * t + r)

                def xt(t):
                    if more:
                        transpose_x(t_base(n) + t, t, 4 * n + 5 + t, x_normed, x_ln)

                def o(t):
                    project(base + 4 + t, t)

                def q(m):
                    if more:
                        query(q_at + m, m)

                scores(n, 0, b, masked, (2, 4) if first else (m_base(n) - 2, m_base(n)))
                if first:
                    pe.wait_ge(wv_in, 16)

                    def batch_values(b_of):
                        m_wait(V_AT + b_of)
                        product(m_bank[b_of % 2][0:SK, :],
                                [(ctx_stage[:, k, b_of * SK:(b_of + 1) * SK], wv_stage[:, k, :])
                                 for k in range(KD)]).then_inc(m_full, 1)

                    batch_values(0)
                    for t in range(TT):
                        xt(t)
                    scores(n, 1, b, False)
                    p(0, 0)
                    p(0, 1)
                    batch_values(1)
                    p(0, 2)
                    scores(n, 2, b, False)
                    p(1, 0)
                    p(1, 1)
                    p(1, 2)
                    scores(n, 3, b, False)
                    pe.wait_ge(t_free, t_base(n) + 4)
                    q(0)
                    p(2, 0)
                    p(2, 1)
                    q(1)
                    p(2, 2)
                    q(2)
                    p(3, 0)
                    p(3, 1)
                    q(3)
                    p(3, 2)
                    return
                for m in range(G):
                    values(base + m, m, b_before, t_base(n) - 2 + min(m, 2))
                    xt(m)
                scores(n, 1, b, False)
                p(0, 0)
                p(0, 1)
                pe.wait_ge(m_free, base + 4)
                o(0)
                p(0, 2)
                if more:
                    o(1)
                scores(n, 2, b, False)
                p(1, 0)
                p(1, 1)
                o(2 if more else 1)
                p(1, 2)
                if more:
                    o(3)
                scores(n, 3, b, False)
                p(2, 0)
                p(2, 1)
                if more:
                    pe.wait_ge(t_free, t_base(n) + 4)
                else:
                    o(2)
                q(0)
                p(2, 2)
                if not more:
                    o(3)
                q(1)
                q(2)
                p(3, 0)
                q(3)
                p(3, 1)
                p(3, 2)

            step(0, 0, 0, True, True, True)
            pe.wait_ge(v_split, B)
            pe.wait_ge(wo_split, 2)
            for b in range(B):
                if b:
                    step(b * BPB, b, b - 1, True, False, True)
                with pe.Fori(b * BPB + 1, (b + 1) * BPB - (b == B - 1)) as n:
                    step(n, b, b, False, False, True)
            step(NB - 1, B - 1, B - 1, False, False, False)
            for m in range(G):
                values(M_LAST + m, m, B - 1, T_P2 - 2 + min(m, 2))
            for t in (0, 1):
                transpose_x(T_P2 + t, t, t + 1, x2_normed, xh)
            pe.wait_ge(m_free, M_LAST + 4)
            for t in range(TT):
                project(M_LAST + 4 + t, t)
                if t < 2:
                    transpose_x(T_P2 + 2 + t, 2 + t, 3 + t, x2_normed, xh)

            def gate_up(n, m, converted=False):
                if m < 2:
                    if not (isinstance(n, int) and n == 0):
                        pe.wait_ge(gu_free, MH * n + m - 1)
                else:
                    pe.wait_ge(gu_free, MH * n + m - 1)
                if converted:
                    pe.wait_ge(raw_used[m % 3], m // 3 + 1)
                for j in range(2):
                    c = (2 * m + j) * P
                    last = product(psum[:, 2 * (m % 2) + j, :],
                                   [(w_gu[:, k, c:c + P], xT2[:, a, k, :]) for k in range(KD) for a in range(2)])
                last.then_inc(gu_full, 1)

            def down(n, t):
                m_wait(M_P2 + 4 * n + t)
                terms = [(hT[:, a, m, t * P:(t + 1) * P], w_d[:, m, :]) for m in range(MH) for a in range(2)]
                for j, (stat, mov) in enumerate(terms):
                    if t == 0 and j % 2 == 0:
                        pe.wait_ge(h_lo, MH * n + j // 2 + 1)
                    last = nc.tensor.matmul(m_bank[t % 2][:, :], stat, mov, start=(j == 0), stop=(j == len(terms) - 1))
                last.then_inc(m_full, 1)

            def ffn(n, more, first=False):
                pe.wait_ge(t_free, T_P2 + 4 * n + 4)
                for m in range(MH):
                    gate_up(n, m, first)
                    if not more and m == MH - 3:
                        pe.wait_ge(w_top_done, 1)
                        nc.tensor.transpose(t_bank[0][0:1, 0:P], w_top[:, :], ident[:, :]).then_inc(w_top_row, 1)

                def xt(t):
                    if more:
                        transpose_x(T_P2 + 4 * n + 4 + t, t, 4 * n + 5 + t, x2_normed, xh)

                xt(0)
                xt(1)
                if first:
                    for slot in range(3):
                        pe.wait_ge(raw_used[slot], len(PARTS) // 3)
                down(n, 0)
                xt(2)
                xt(3)
                for t in range(1, TT):
                    down(n, t)

            ffn(0, True, True)
            with pe.Fori(1, NB - 1) as n:
                ffn(n, True)
            ffn(NB - 1, False)

            with pe.If(too_wide(pe)):
                with pe.Fori(0, NT) as n:
                    pe.wait_ge(wide_normed, n + 1)
                    for k in range(KD):
                        last = nc.tensor.transpose(t_bank[0][:, k * P:(k + 1) * P], wide_xh[:, k * P:(k + 1) * P],
                                                   ident[:, :])
                    last.then_inc(wide_t, 1)
                    pe.wait_ge(wide_xt_ready, n + 1)
                    for m in range(MH):
                        if m >= 2:
                            pe.wait_ge(wide_hid, MH * n + m - 1)
                        for j in range(2):
                            last = product(psum[:, 2 * (m % 2) + j, 0:P],
                                           [(wide_gu[:, k, j, m * P:(m + 1) * P], wide_xT[:, k, :])
                                            for k in range(KD)])
                        last.then_inc(wide_gu_full, 1)
                    pe.wait_ge(wide_hid, MH * n + MH)
                    product(m_bank[0][:, :], [(wide_h[:, m, :], wide_d[:, m, :]) for m in range(MH)])\
                        .then_inc(wide_down, 1)


def kernel(**inputs):
    import numpy as np
    import concourse.bacc as bacc
    from concourse.bass_utils import run_bass_kernel_spmd as run

    def t(name):
        return np.ascontiguousarray(np.asarray(inputs[name]).T)

    c = np.asarray(inputs["ctx_1024"])
    x = np.ascontiguousarray(inputs["x"])
    arrays = {
        "x": x,
        "ctx_t": np.ascontiguousarray(c.reshape(-1, c.shape[2]).T),
        "g_xattn": np.ascontiguousarray(np.broadcast_to(np.asarray(inputs["g_xattn"]).reshape(1, 1), (128, 1))),
        "g_ffn": np.ascontiguousarray(np.broadcast_to(np.asarray(inputs["g_ffn"]).reshape(1, 1), (128, 1))),
        "wq_t": t("L0_xattn_Wq"), "wk_t": t("L0_xattn_Wk"), "wv_t": t("L0_xattn_Wv"), "wo_t": t("L0_xattn_Wo"),
        "w_gate_t": t("L0_ffn_w_gate"), "w_up_t": t("L0_ffn_w_up"), "w_down_t": t("L0_ffn_w_down"),
    }
    nc = bacc.Bacc("TRN2", target_bir_lowering=False, num_devices=1,
                   dynamic_dma_scratch_size=1024)
    args = [nc.dram_tensor(n, a.shape, mybir.dt.from_np(a.dtype), kind="ExternalInput").ap() for n, a in arrays.items()]
    args.append(nc.dram_tensor("x_mid", (x.shape[0] * x.shape[1], x.shape[2]), mybir.dt.float32, kind="Internal").ap())
    args.append(nc.dram_tensor("out", x.shape, mybir.dt.float32, kind="ExternalOutput").ap())
    flamingo_gated_block(nc, *args)
    r = run(nc, [arrays], core_ids=[0])
    return r.results[0]["out"]
```
